# Optimizing a Trainium2 kernel written in Bass

```python
import numpy as np
import jax
import jax.numpy as jnp

def _softmax(x, axis=-1):
    return jax.nn.softmax(x, axis=axis)

def _gelu(x):
    return jax.nn.gelu(x, approximate=True)

def _silu(x):
    return jax.nn.silu(x)

def _sigmoid(x):
    return jax.nn.sigmoid(x)

def _layernorm(x, axis=-1, eps=1e-05):
    m = jnp.mean(x, axis=axis, keepdims=True)
    v = jnp.var(x, axis=axis, keepdims=True)
    return (x - m) / jnp.sqrt(v + eps)

def _scatter_add(tgt, idx, src, axis=0):
    return tgt.at[idx].add(src)

def _segment_sum(src, seg, n):
    return jax.ops.segment_sum(src, seg, n)
kernel_name = 'mk_gnn_resnorm_d2_gnn_r8_72dfe0'

def setup_inputs(seed: int=0):
    np.random.seed(seed)
    _w = jnp.asarray

    def _rec_inputs():
        import jax
        import jax.numpy as jnp
        _gk = jax.random.key(seed)
        x = -0.000202 + 1 * jax.random.normal(jax.random.fold_in(_gk, 1), (6250, 128), jnp.float32)
        src = jax.random.randint(jax.random.fold_in(_gk, 2), (100000,), 0, 6250, jnp.int32)
        dst = jnp.minimum((6250 * jax.random.uniform(jax.random.fold_in(_gk, 3), (100000,)) ** 2.0).astype(jnp.int32), 49999)
        _o = jnp.argsort(dst, stable=True)
        src = src[_o]
        dst = dst[_o]
        edge_attr_128 = -6.47781e-05 + 0.999943 * jax.random.normal(jax.random.fold_in(_gk, 11), (100000, 128), jnp.float32)
        edge_weight = 0.000614103 + 0.999867 * jax.random.normal(jax.random.fold_in(_gk, 13), (100000,), jnp.float32)
        return (x, src, dst, edge_attr_128, edge_weight)
    x, src, dst, edge_attr_128, edge_weight = _rec_inputs()

    def _L0_gnn_setup():
        import jax, jax.numpy as jnp
        import numpy as np
        N_NODES = 6250
        key = jax.random.key(seed)
        ks = jax.random.split(key, 8)
        x = jax.random.normal(ks[0], (N_NODES, 128), dtype=jnp.float32)
        edge_attr = jax.random.normal(ks[1], (200000, 128), dtype=jnp.float32)
        u = jax.random.normal(ks[2], (1, 16), dtype=jnp.float32)
        d_in = 128 + 128 + 16
        W1 = jax.random.normal(ks[3], (d_in, 1024), dtype=jnp.float32) * (1.0 / np.sqrt(d_in))
        b1 = jnp.zeros((1024,), dtype=jnp.float32)
        W2 = jax.random.normal(ks[4], (1024, 128), dtype=jnp.float32) * (1.0 / np.sqrt(1024))
        b2 = jnp.zeros((128,), dtype=jnp.float32)
        edge_index = jax.random.randint(ks[5], (2, 200000), 0, N_NODES, dtype=jnp.int64)
        return {'x': x, 'edge_attr': edge_attr, 'u': u, 'W1': W1, 'b1': b1, 'W2': W2, 'b2': b2, 'edge_index': edge_index}
    _L0_gnn_all = _L0_gnn_setup()
    _L0_gnn_in = {k: v for k, v in _L0_gnn_all.items() if k in ('u', 'W1', 'b1', 'W2', 'b2')}
    del _L0_gnn_all

    def _L1_gnn_setup():
        import jax, jax.numpy as jnp
        import numpy as np
        N, F, H, C = (6250, 128, 4, 32)
        E = 100000
        D = H * C

        def _tconv(x, src, dst, ea, Wq, bq, Wk, bk, Wv, bv, We, Ws, bs):
            n = x.shape[0]
            q = (x @ Wq + bq).reshape(n, H, C)
            k = (x @ Wk + bk).reshape(n, H, C)
            v = (x @ Wv + bv).reshape(n, H, C)
            e = (ea @ We).reshape(-1, H, C)
            kj = k[src] + e
            alpha = jnp.einsum('ehc,ehc->eh', q[dst], kj) / jnp.sqrt(jnp.float32(C))
            amax = jax.ops.segment_max(alpha, dst, num_segments=n)
            ex = jnp.exp(alpha - amax[dst])
            denom = jax.ops.segment_sum(ex, dst, num_segments=n)
            w = ex / (denom[dst] + 1e-16)
            msg = (v[src] + e) * w[:, :, None]
            out = jax.ops.segment_sum(msg, dst, num_segments=n).reshape(n, D)
            return out + x @ Ws + bs
        key = jax.random.key(seed)
        ks = jax.random.split(key, 24)
        s = lambda i, shape, scale: jax.random.normal(ks[i], shape, dtype=jnp.float32) * scale
        inp = {'x': s(0, (N, F), 1.0), 'edge_index': jax.random.randint(ks[1], (2, E), 0, N), 'edge_attr': s(2, (E,), 1.0), 'Wq1': s(3, (F, D), 1.0 / np.sqrt(F)), 'bq1': jnp.zeros((D,), jnp.float32), 'Wk1': s(4, (F, D), 1.0 / np.sqrt(F)), 'bk1': jnp.zeros((D,), jnp.float32), 'Wv1': s(5, (F, D), 1.0 / np.sqrt(F)), 'bv1': jnp.zeros((D,), jnp.float32), 'We1': s(6, (1, D), 1.0), 'Ws1': s(7, (F, D), 1.0 / np.sqrt(F)), 'bs1': jnp.zeros((D,), jnp.float32), 'Wq2': s(8, (D, D), 1.0 / np.sqrt(D)), 'bq2': jnp.zeros((D,), jnp.float32), 'Wk2': s(9, (D, D), 1.0 / np.sqrt(D)), 'bk2': jnp.zeros((D,), jnp.float32), 'Wv2': s(10, (D, D), 1.0 / np.sqrt(D)), 'bv2': jnp.zeros((D,), jnp.float32), 'We2': s(11, (1, D), 1.0), 'Ws2': s(12, (D, D), 1.0 / np.sqrt(D)), 'bs2': jnp.zeros((D,), jnp.float32)}
        return inp
    _L1_gnn_all = _L1_gnn_setup()
    _L1_gnn_in = {k: v for k, v in _L1_gnn_all.items() if k in ('Wq1', 'bq1', 'Wk1', 'bk1', 'Wv1', 'bv1', 'We1', 'Ws1', 'bs1', 'Wq2', 'bq2', 'Wk2', 'bk2', 'Wv2', 'bv2', 'We2', 'Ws2', 'bs2')}
    del _L1_gnn_all
    return {'x': x, 'src': src, 'dst': dst, 'edge_attr_128': edge_attr_128, 'edge_weight': edge_weight, 'L0_gnn_u': _L0_gnn_in['u'], 'L0_gnn_W1': _L0_gnn_in['W1'], 'L0_gnn_b1': _L0_gnn_in['b1'], 'L0_gnn_W2': _L0_gnn_in['W2'], 'L0_gnn_b2': _L0_gnn_in['b2'], 'L1_gnn_Wq1': _L1_gnn_in['Wq1'], 'L1_gnn_bq1': _L1_gnn_in['bq1'], 'L1_gnn_Wk1': _L1_gnn_in['Wk1'], 'L1_gnn_bk1': _L1_gnn_in['bk1'], 'L1_gnn_Wv1': _L1_gnn_in['Wv1'], 'L1_gnn_bv1': _L1_gnn_in['bv1'], 'L1_gnn_We1': _L1_gnn_in['We1'], 'L1_gnn_Ws1': _L1_gnn_in['Ws1'], 'L1_gnn_bs1': _L1_gnn_in['bs1'], 'L1_gnn_Wq2': _L1_gnn_in['Wq2'], 'L1_gnn_bq2': _L1_gnn_in['bq2'], 'L1_gnn_Wk2': _L1_gnn_in['Wk2'], 'L1_gnn_bk2': _L1_gnn_in['bk2'], 'L1_gnn_Wv2': _L1_gnn_in['Wv2'], 'L1_gnn_bv2': _L1_gnn_in['bv2'], 'L1_gnn_We2': _L1_gnn_in['We2'], 'L1_gnn_Ws2': _L1_gnn_in['Ws2'], 'L1_gnn_bs2': _L1_gnn_in['bs2']}

def reference(x, src, dst, edge_attr_128, edge_weight, L0_gnn_u, L0_gnn_W1, L0_gnn_b1, L0_gnn_W2, L0_gnn_b2, L1_gnn_Wq1, L1_gnn_bq1, L1_gnn_Wk1, L1_gnn_bk1, L1_gnn_Wv1, L1_gnn_bv1, L1_gnn_We1, L1_gnn_Ws1, L1_gnn_bs1, L1_gnn_Wq2, L1_gnn_bq2, L1_gnn_Wk2, L1_gnn_bk2, L1_gnn_Wv2, L1_gnn_bv2, L1_gnn_We2, L1_gnn_Ws2, L1_gnn_bs2):
    import jax
    import jax.numpy as jnp

    def _L0_gnn_ref(x, edge_attr, u, W1, b1, W2, b2, edge_index):
        import jax, jax.numpy as jnp
        import numpy as np
        N_NODES = 6250
        n = x.shape[0]
        recv_idx = edge_index[1]
        recv_agg = jax.ops.segment_sum(edge_attr, recv_idx, num_segments=n)
        u_b = jnp.broadcast_to(u, (n, u.shape[-1]))
        collected = jnp.concatenate([recv_agg, x, u_b], axis=-1)
        h = jax.nn.relu(collected @ W1 + b1)
        updated_nodes = h @ W2 + b2
        return updated_nodes

    def _L1_gnn_ref(x, edge_index, edge_attr, Wq1, bq1, Wk1, bk1, Wv1, bv1, We1, Ws1, bs1, Wq2, bq2, Wk2, bk2, Wv2, bv2, We2, Ws2, bs2):
        import jax, jax.numpy as jnp
        import numpy as np
        N, F, H, C = (6250, 128, 4, 32)
        E = 100000
        D = H * C

        def _tconv(x, src, dst, ea, Wq, bq, Wk, bk, Wv, bv, We, Ws, bs):
            n = x.shape[0]
            q = (x @ Wq + bq).reshape(n, H, C)
            k = (x @ Wk + bk).reshape(n, H, C)
            v = (x @ Wv + bv).reshape(n, H, C)
            e = (ea @ We).reshape(-1, H, C)
            kj = k[src] + e
            alpha = jnp.einsum('ehc,ehc->eh', q[dst], kj) / jnp.sqrt(jnp.float32(C))
            amax = jax.ops.segment_max(alpha, dst, num_segments=n)
            ex = jnp.exp(alpha - amax[dst])
            denom = jax.ops.segment_sum(ex, dst, num_segments=n)
            w = ex / (denom[dst] + 1e-16)
            msg = (v[src] + e) * w[:, :, None]
            out = jax.ops.segment_sum(msg, dst, num_segments=n).reshape(n, D)
            return out + x @ Ws + bs
        src, dst = (edge_index[0], edge_index[1])
        ea = edge_attr.reshape(-1, 1)
        h = _tconv(x, src, dst, ea, Wq1, bq1, Wk1, bk1, Wv1, bv1, We1, Ws1, bs1)
        h = jax.nn.relu(h)
        h = _tconv(h, src, dst, ea, Wq2, bq2, Wk2, bk2, Wv2, bv2, We2, Ws2, bs2)
        return jax.nn.relu(h)
    edge_index = jnp.stack([src, dst])
    x = _layernorm(x + _L0_gnn_ref(x, edge_attr_128, L0_gnn_u, L0_gnn_W1, L0_gnn_b1, L0_gnn_W2, L0_gnn_b2, edge_index), axis=-1)
    x = _layernorm(x + _L1_gnn_ref(x, edge_index, edge_weight, L1_gnn_Wq1, L1_gnn_bq1, L1_gnn_Wk1, L1_gnn_bk1, L1_gnn_Wv1, L1_gnn_bv1, L1_gnn_We1, L1_gnn_Ws1, L1_gnn_bs1, L1_gnn_Wq2, L1_gnn_bq2, L1_gnn_Wk2, L1_gnn_bk2, L1_gnn_Wv2, L1_gnn_bv2, L1_gnn_We2, L1_gnn_Ws2, L1_gnn_bs2), axis=-1)
    return x

_drawn_inputs = setup_inputs


def setup_inputs(seed=0):
    import zlib

    import numpy as np

    out = dict(_drawn_inputs(seed))
    spreads = {'L0_gnn_b1': (0.0, 0.1),
     'L0_gnn_b2': (0.0, 0.1),
     'L1_gnn_bq1': (0.0, 0.335),
     'L1_gnn_bk1': (0.0, 0.8),
     'L1_gnn_bv1': (0.0, 0.1),
     'L1_gnn_bs1': (0.0, 0.1),
     'L1_gnn_bq2': (0.0, 0.1),
     'L1_gnn_bk2': (0.0, 0.8),
     'L1_gnn_bv2': (0.0, 0.1),
     'L1_gnn_bs2': (0.0, 0.1)}
    factors = {}
    for name, (base, spread) in spreads.items():
        noise = np.random.default_rng([zlib.crc32(name.encode()), seed]).standard_normal(out[name].shape)
        drawn = base * np.exp(spread * noise) if base else spread * noise
        out[name] = jnp.asarray(drawn.astype(out[name].dtype))
    for name, factor in factors.items():
        out[name] = (out[name] * factor).astype(out[name].dtype)
    return out
```

```python
from contextlib import ExitStack

import concourse.bass as bass
import concourse.mybir as mybir
import numpy as np

F32 = mybir.dt.float32
BF16 = mybir.dt.bfloat16
I32 = mybir.dt.int32
ALU = mybir.AluOpType
ACT = mybir.ActivationFunctionType
AX = mybir.AxisListType

P = 128
NODES, EDGES, FEAT, HEADS = 6250, 100000, 128, 4
HC = FEAT // HEADS
GLOB, HID = 16, 1024
NW = -(-NODES // P)
ROWS = NW * P
NT = -(-EDGES // P)
BODY = 4
HALF = BODY // 2
MIN_BODIES = 2
TABLE = NT + MIN_BODIES * BODY + 2
TB = -(-NT // P)
NCH = HID // P
SLOTS = 4
QW = FEAT + HEADS
HP = HC + 2
PW = HEADS * HP
OUTW = 7
BIG = float(2 ** 100)
SCALE = float(HC) ** -0.5
EPS = 1e-5
MAXB = NW * (-(-(NT + 1) // BODY)) + NW * MIN_BODIES


def repeat(ap, axis, n):
    shape = list(ap.shape)
    shape[axis] = n
    return ap.broadcast_to(shape)


def build(nc, x, x_t, src_t, dst_t, dst_r, ew_t, edge_attr, u_t, w1, b1_t, w2, b2,
          wcat1, bcat1, we1, wcat2, bcat2, we2, out):
    kv = [nc.dram_tensor(f"kv{n}", [ROWS, 2 * FEAT], F32).ap() for n in (1, 2)]
    ctx = ExitStack()
    with ctx:
        def sb(name, shape, dt=F32):
            return ctx.enter_context(nc.sbuf_tensor(name, shape, dt))

        def pb(name, shape, dt=F32):
            return ctx.enter_context(nc.psum_tensor(name, shape, dt))

        def sem(name):
            return ctx.enter_context(nc.semaphore(name))

        src_sb = sb("src_sb", [P, TABLE], I32)
        dst_sb = sb("dst_sb", [P, TABLE])
        ew_sb = sb("ew_sb", [P, TABLE])
        dst_i = sb("dst_i", [P, TABLE], I32)
        tab = sb("tab", [1, 3, NW + 2], I32)
        wbase = sb("wbase", [P, NW + 1])
        iota_n = sb("iota_n", [P, P])
        ident = sb("ident", [P, P])
        identb = sb("identb", [P, P], BF16)
        ones = sb("ones", [P, P])
        sel = sb("sel", [P, 2 * HEADS, P], BF16)
        q_all = sb("q_all", [P, NW + 1, QW])
        s_all = sb("s_all", [P, NW + 1, FEAT])
        x1 = sb("x1", [P, NW, FEAT])
        agg_all = sb("agg_all", [P, NW, FEAT])
        wcat = [sb(f"wcat{n}", [P, 4 * FEAT]) for n in (0, 1)]
        bcat = [sb(f"bcat{n}", [P, 4 * FEAT]) for n in (0, 1)]
        web = [sb(f"web{n}", [P, FEAT]) for n in (0, 1)]
        onehot = [sb(f"onehot{s}", [P, HALF, P]) for s in (0, 1)]
        ring = sb("ring", [P, SLOTS, BODY, 2 * FEAT])
        epst = sb("epst", [P, 1])

        stats_done = sem("stats_done")

        bank = [pb(f"bank{n}", [P, 512]) for n in range(8)]

        def tile_of(i, w_row, eng):
            first_body, first_tile = w_row
            return nc.s_assert_within(
                first_tile + (i - first_body) * BODY, 0, TABLE - BODY,
                skip_runtime_bounds_check_because="the bodies of a window end at most two bodies past its last tile")

        def bodies(eng, w):
            a = eng.value_load(tab[0:1, 0, bass.ds(w, 1)], min_val=0, max_val=MAXB)
            b = eng.value_load(tab[0:1, 0, bass.ds(w + 1, 1)], min_val=0, max_val=MAXB)
            t = eng.value_load(tab[0:1, 1, bass.ds(w, 1)], min_val=0, max_val=NT)
            return a, b, t

        bounds_stage(nc, ctx, locals())
        collect_stage(nc, locals())
        update_stage(nc, locals())
        attend_stage(nc, locals(), 0)
        attend_stage(nc, locals(), 1)


def bounds_stage(nc, ctx, m):
    (src_sb, dst_sb, dst_i, ew_sb, tab, wbase, iota_n, ident, identb, ones, sel, q_all, x1, wcat, bcat,
     web, bank, s_all, epst) = (m[k] for k in (
        "src_sb", "dst_sb", "dst_i", "ew_sb", "tab", "wbase", "iota_n", "ident", "identb", "ones", "sel",
        "q_all", "x1", "wcat", "bcat", "web", "bank", "s_all", "epst"))
    W1 = NW + 1
    FAR = 1024.0
    with ExitStack() as c:
        def sb(name, shape, dt=F32):
            return c.enter_context(nc.sbuf_tensor(name, shape, dt))

        dst_rows = sb("dst_rows", [P, TB, P], I32)
        low = sb("low", [P, TB])
        high = sb("high", [P, TB])
        tile_no = sb("tile_no", [P, TB])
        wrow = sb("wrow", [P, W1])
        wend = sb("wend", [P, W1])
        below = sb("below", [P, TB, W1])
        above = sb("above", [P, TB, W1])
        reach = sb("reach", [P, 2, W1])
        reach_c = sb("reach_c", [2 * W1, 1])
        row = sb("row", [1, 2 * W1])
        first = sb("first", [1, W1])
        count = sb("count", [1, W1])
        count_i = sb("count_i", [1, W1], I32)
        zrow = sb("zrow", [1, W1])
        cum = sb("cum", [1, W1 + 1])
        loaded = c.enter_context(nc.semaphore("b_loaded"))
        made = c.enter_context(nc.semaphore("b_made"))
        steps = c.enter_context(nc.semaphore("b_steps"))
        turned = c.enter_context(nc.semaphore("b_turned"))
        block = c.enter_context(nc.Block())
        blank = [0]

        @block.gpsimd
        def _(pool):
            pool.iota(iota_n[:, :], [[1, P]], base=0, channel_multiplier=0,
                      allow_small_or_imprecise_dtypes=True).then_inc(made, 1)
            pool.iota(wbase[:, :], [[P, W1]], base=0, channel_multiplier=0,
                      allow_small_or_imprecise_dtypes=True).then_inc(made, 1)
            pool.iota(tile_no[:, :], [[P, TB]], base=0, channel_multiplier=1,
                      allow_small_or_imprecise_dtypes=True).then_inc(made, 1)
            pool.memset(ones[:, :], 1.0).then_inc(made, 1)
            pool.memset(sel[:, :, :], 0.0).then_inc(made, 1)
            pool.wait_ge(made, 5)
            pool.affine_select(out=ident[:, :], in_=ones[:, :], compare_op=ALU.is_equal, fill=0.0,
                               base=0, pattern=[[-1, P]], channel_multiplier=1).then_inc(made, 1)
            pool.affine_select(out=sel[:, :, :], in_=sel[:, :, :], compare_op=ALU.not_equal, fill=1.0,
                               base=0, pattern=[[-1, 2 * HEADS], [0, P]], channel_multiplier=1).then_inc(made, 1)
            pool.wait_ge(made, 7)
            pool.tensor_copy(identb[:, :], ident[:, :]).then_inc(made, 1)
            pool.memset(q_all[:, NW, :], 0.0).then_inc(made, 1)
            pool.memset(epst[:, :], EPS).then_inc(made, 1)
            pool.wait_ge(made, 10)

        @block.sync
        def _(sp):
            sp.dma_start(dst_i[:, :], m["dst_t"]).then_inc(loaded, 16)
            sp.wait_ge(steps, 1)
            full = NT // P * P
            sp.dma_start(dst_rows[:, 0:NT // P, :],
                         m["dst_r"][0:full, :].rearrange("(b p) e -> p b e", p=P)).then_inc(loaded, 16)
            sp.dma_start(dst_rows[0:NT - full, NT // P, :], m["dst_r"][full:NT, :]).then_inc(loaded, 16)
            sp.dma_start(src_sb[:, :], m["src_t"]).then_inc(loaded, 16)
            sp.dma_start(ew_sb[:, :], m["ew_t"]).then_inc(loaded, 16)
            for n, (wc, bc, we) in enumerate((("wcat1", "bcat1", "we1"), ("wcat2", "bcat2", "we2"))):
                sp.dma_start(wcat[n][:, :], m[wc]).then_inc(loaded, 16)
                sp.dma_start(bcat[n][:, :], repeat(m[bc], 0, P)).then_inc(loaded, 16)
                sp.dma_start(web[n][:, :], repeat(m[we], 0, P)).then_inc(loaded, 16)
            sp.wait_ge(loaded, 16 * 11)

        @block.vector
        def _(dve):
            n = [0]

            def step(ins):
                n[0] += 1
                ins.then_inc(steps, 1)
                dve.wait_ge(steps, n[0])

            step(dve.memset(dst_rows[:, :, :], 1 << 20))
            dve.wait_ge(loaded, 16 * 11)
            dve.wait_ge(made, 10)
            step(dve.tensor_copy(dst_sb[:, :], dst_i[:, :]))
            for b in bcat:
                step(dve.tensor_scalar(b[:, 0:FEAT], b[:, 0:FEAT], SCALE, None, ALU.mult))
            step(dve.tensor_reduce(low[:, :], dst_rows[:, :, :], AX.X, ALU.min))
            step(dve.tensor_reduce(high[:, :], dst_rows[:, :, :], AX.X, ALU.max))
            step(dve.tensor_scalar(wend[:, :], wbase[:, :], float(P), None, ALU.add))
            low_b = repeat(low[:, :].unsqueeze(2), 2, W1)
            high_b = repeat(high[:, :].unsqueeze(2), 2, W1)
            step(dve.tensor_tensor(below[:, :, :], repeat(wend[:, :].unsqueeze(1), 1, TB), low_b, ALU.is_gt))
            step(dve.tensor_tensor(above[:, :, :], repeat(wbase[:, :].unsqueeze(1), 1, TB), high_b, ALU.is_le))
            step(dve.tensor_tensor(below[:, :, :], below[:, :, :], above[:, :, :], ALU.mult))
            step(dve.tensor_scalar(high[:, :], tile_no[:, :], -1.0, FAR, ALU.mult, ALU.add))
            step(dve.tensor_scalar(low[:, :], tile_no[:, :], 1.0, None, ALU.add))
            step(dve.tensor_tensor(above[:, :, :], below[:, :, :], high_b, ALU.mult))
            step(dve.tensor_tensor(below[:, :, :], below[:, :, :], low_b, ALU.mult))
            step(dve.tensor_reduce(reach[:, 0, :], below[:, :, :].rearrange("p b w -> p w b"), AX.X, ALU.max))
            step(dve.tensor_reduce(reach[:, 1, :], above[:, :, :].rearrange("p b w -> p w b"), AX.X, ALU.max))
            dve.wait_ge(turned, 1)
            step(dve.tensor_reduce(reach_c[:, :], bank[0][0:2 * W1, 0:P], AX.X, ALU.max))
            blank[0] = n[0]
            dve.wait_ge(turned, 2)
            step(dve.tensor_copy(row[:, :], bank[1][0:1, 0:2 * W1]))
            step(dve.tensor_scalar(first[:, :], row[:, W1:2 * W1], -1.0, FAR, ALU.mult, ALU.add))
            step(dve.tensor_scalar(first[:, :], first[:, :], float(NT - 1), None, ALU.min))
            step(dve.tensor_tensor(count[:, :], row[:, 0:W1], first[:, :], ALU.subtract))
            step(dve.tensor_scalar(count[:, :], count[:, :], float(BODY - 1), float(MIN_BODIES * BODY),
                                   ALU.add, ALU.max))
            step(dve.tensor_copy(count_i[:, :], count[:, :]))
            step(dve.tensor_scalar(count_i[:, :], count_i[:, :], BODY.bit_length() - 1, None,
                                   ALU.arith_shift_right))
            step(dve.tensor_copy(count[:, :], count_i[:, :]))
            step(dve.memset(zrow[:, :], 0.0))
            step(dve.memset(cum[:, 0:1], 0.0))
            step(dve.tensor_tensor_scan(cum[:, 1:W1 + 1], zrow[:, :], count[:, :], 0.0, ALU.add, ALU.add))
            step(dve.tensor_copy(tab[0:1, 0, 0:W1 + 1], cum[:, :]))
            step(dve.tensor_copy(tab[0:1, 1, 0:W1], first[:, :]))
            step(dve.tensor_scalar(tab[0:1, 2, 0:W1], cum[:, 1:W1 + 1], -1.0, None, ALU.add))

        @block.tensor
        def _(pe):
            pe.wait_ge(made, 10)
            pe.wait_ge(steps, blank[0] - 1)
            pe.transpose(bank[0][0:2 * W1, 0:P], reach[:, :, :].rearrange("p a w -> p (a w)"),
                         ident[:, :]).then_inc(turned, 1)
            pe.wait_ge(steps, blank[0])
            pe.matmul(bank[1][0:1, 0:2 * W1], reach_c[:, :], ident[0:2 * W1, 0:2 * W1],
                      start=True, stop=True).then_inc(turned, 1)


def branch4(eng, i, emit):
    k = eng.snap(i % SLOTS)
    with eng.If(k < 2):
        with eng.If(k < 1):
            emit(0)
        with eng.Else():
            emit(1)
    with eng.Else():
        with eng.If(k < 3):
            emit(2)
        with eng.Else():
            emit(3)


def fill_ring(eng, m, windows, lag, start, landed, per_body, ready):
    bodies, tile_of = m["bodies"], m["tile_of"]

    def tell(at):
        def wait(k):
            eng.wait_ge(landed[k], (at // SLOTS) * per_body)
            eng.sem_inc(ready, 1)
        branch4(eng, at, wait)

    def one(i, row):
        t = eng.snap(tile_of(i, row, eng))
        branch4(eng, i, lambda k: start(k, i, t))
        tell(i + SLOTS - lag)

    with eng.Fori(0, windows) as w:
        a, b, t0 = bodies(eng, w)
        with eng.Fori(a, b) as i:
            one(i, (a, t0))
    total = eng.value_load(m["tab"][0:1, 0, windows:windows + 1], min_val=SLOTS, max_val=MAXB)
    return total, one, tell


def in_halves(eng, m, first, step, end):
    first()
    with eng.Fori(0, NW) as w:
        a, _, t0 = m["bodies"](eng, w)
        last = eng.value_load(m["tab"][0:1, 2, bass.ds(w, 1)], min_val=1, max_val=MAXB)
        t_next = eng.value_load(m["tab"][0:1, 1, bass.ds(w + 1, 1)], min_val=0, max_val=NT)
        with eng.Fori(a, last) as i:
            step(0, (i, w, (a, t0)), (i, w, (a, t0)))
            step(1, (i, w, (a, t0)), (i + 1, w, (a, t0)))
        step(0, (last, w, (a, t0)), (last, w, (a, t0)))
        step(1, (last, w, (a, t0)), (last + 1, w + 1, (last + 1, t_next)))
        end(w, last + 1)


def make_onehot(dve, m, s, now):
    i, w, row = now
    t = m["tile_of"](i, row, dve)
    return dve.scalar_tensor_tensor(
        m["onehot"][s][:, :, :], repeat(m["iota_n"][:, :].unsqueeze(1), 1, HALF),
        m["wbase"][:, bass.ds(w, 1)],
        repeat(m["dst_sb"][:, bass.ds(t + HALF * s, HALF)].unsqueeze(2), 2, P), ALU.add, ALU.is_equal)


def collect_stage(nc, m):
    agg_all, onehot, ring, bank = (m[k] for k in ("agg_all", "onehot", "ring", "bank"))
    edge_rows = m["edge_attr"].rearrange("(t p) f -> p t f", p=P)
    LAG = 2
    with ExitStack() as c:
        acc = c.enter_context(nc.sbuf_tensor("c_acc", [P, FEAT], F32))
        landed = [c.enter_context(nc.semaphore(f"c_landed{k}")) for k in range(SLOTS)]
        rows_ready, slot_free, hot, summed, added, cleared, kept = (
            c.enter_context(nc.semaphore(n)) for n in
            ("c_rows_ready", "c_slot_free", "c_hot", "c_summed", "c_added", "c_cleared", "c_kept"))
        block = c.enter_context(nc.Block())

        @block.sync
        def _(sp):
            def load(k, i, t):
                sp.wait_ge(slot_free, i + 1)
                sp.dma_start(ring[:, k, :, 0:FEAT], edge_rows[:, bass.ds(t, BODY), :]).then_inc(landed[k], 16)

            sp.sem_inc(slot_free, SLOTS)
            total, _, tell = fill_ring(sp, m, NW, LAG, load, landed, 16, rows_ready)
            for back in range(LAG, 0, -1):
                tell(total + SLOTS - back)

        @block.vector
        def _(dve):
            def first():
                dve.memset(acc[:, :], 0.0).then_inc(cleared, 1)
                make_onehot(dve, m, 0, (0, 0, (0, dve.value_load(m["tab"][0:1, 1, 0:1], min_val=0, max_val=NT)))
                            ).then_inc(hot, 1)

            def step(s, now, ahead):
                i, w, _ = now
                dve.wait_ge(summed, 2 * i + s)
                make_onehot(dve, m, 1 - s, ahead).then_inc(hot, 1)
                dve.wait_ge(summed, 2 * i + s + 1)
                dve.wait_ge(cleared, w + 1)
                dve.wait_ge(added, 2 * i + s)
                dve.tensor_tensor(acc[:, :], acc[:, :], bank[s][:, 0:FEAT], ALU.add).then_inc(added, 1)

            def end(w, b):
                dve.wait_ge(added, 2 * b)
                dve.tensor_copy(agg_all[:, bass.ds(w, 1), :].rearrange("p a f -> p (a f)"), acc[:, :]).then_inc(kept, 1)
                dve.wait_ge(kept, w + 1)
                dve.memset(acc[:, :], 0.0).then_inc(cleared, 1)

            in_halves(dve, m, first, step, end)

        @block.tensor
        def _(pe):
            with pe.Fori(0, NW) as w:
                a, b, _ = m["bodies"](pe, w)
                with pe.Fori(a, b) as i:
                    for s in (0, 1):
                        if s == 0:
                            pe.wait_ge(rows_ready, i + 1 + LAG)
                        pe.wait_ge(hot, 2 * i + s + 1)
                        for k in range(HALF):
                            rows = ring[:, bass.ds(i % SLOTS, 1), HALF * s + k, 0:FEAT].rearrange("p a f -> p (a f)")
                            last = pe.matmul(bank[s][:, 0:FEAT], onehot[s][:, k, :], rows,
                                             start=(k == 0), stop=(k == HALF - 1))
                        last.then_inc(summed, 1)
                    pe.wait_ge(summed, 2 * i + 2)
                    pe.sem_inc(slot_free, 1)


def store_projections(dve, chain, m, layer, w, proj, kv_out, prod):
    q_all, s_all, bcat, web = m["q_all"], m["s_all"], m["bcat"][layer], m["web"][layer]
    here = bass.ds(w, 1)
    chain(dve.tensor_tensor(kv_out[:, :], proj[:, FEAT:3 * FEAT], bcat[:, FEAT:3 * FEAT], ALU.add))
    chain(dve.scalar_tensor_tensor(q_all[:, here, 0:FEAT].rearrange("p a f -> p (a f)"), proj[:, 0:FEAT], SCALE,
                                   bcat[:, 0:FEAT], ALU.mult, ALU.add), wait=True)
    chain(dve.tensor_tensor(s_all[:, here, :].rearrange("p a f -> p (a f)"), proj[:, 3 * FEAT:4 * FEAT],
                            bcat[:, 3 * FEAT:4 * FEAT], ALU.add))
    chain(dve.tensor_tensor(prod, q_all[:, here, 0:FEAT].rearrange("p a f -> p (a f)"), web[:, :], ALU.mult), wait=True)
    chain(dve.tensor_reduce(q_all[:, here, FEAT:QW].rearrange("p a h -> p (a h)"),
                            prod.rearrange("p (h c) -> p h c", h=HEADS), AX.X, ALU.add), wait=True)


class Chain:

    def __init__(self, eng, sem, per, turn):
        self.eng, self.sem, self.base, self.n, self.per = eng, sem, turn * per, 0, per

    def __call__(self, ins, wait=False):
        ins.then_inc(self.sem, 1)
        self.n += 1
        if wait:
            self.eng.wait_ge(self.sem, self.base + self.n)


def update_stage(nc, m):
    agg_all, x1, bank, ident = (m[k] for k in ("agg_all", "x1", "bank", "ident"))
    with ExitStack() as c:
        def sb(name, shape, dt=F32):
            return c.enter_context(nc.sbuf_tensor(name, shape, dt))

        w1a = sb("w1a", [FEAT, HID])
        w1x = sb("w1x", [FEAT, HID])
        w1u = sb("w1u", [GLOB, HID])
        u_c = sb("u_c", [GLOB, 1])
        b1_c = sb("b1_c", [P, NCH])
        hbias = sb("hbias", [P, NCH])
        w2c = sb("w2c", [P, NCH, FEAT])
        b2b = sb("b2b", [P, FEAT])
        x_tw = sb("x_tw", [FEAT, 2, P])
        agg_w = sb("agg_w", [P, FEAT])
        agg_t = sb("agg_t", [FEAT, P])
        hid_t = sb("hid_t", [P, NCH, P])
        res = sb("res", [P, FEAT])
        stats = sb("stats", [P, 6])
        mv = sb("mv", [P, 2])
        std = sb("std", [P, 1])
        xs = sb("xs", [P, FEAT])
        xs_t = sb("xs_t", [FEAT, P])
        kv_out = sb("kv_out", [P, 2 * FEAT])
        prod = sb("u_prod", [P, FEAT])
        names = ("u_loaded", "u_xt0", "u_xt1", "u_bias_ps", "u_bias", "u_aggw", "u_aggt_ps", "u_aggt", "u_hid_ps",
                 "u_hid", "u_y", "u_dve", "u_std", "u_xst_ps", "u_xst", "u_proj", "u_kept", "u_stored")
        (loaded, xt0, xt1, bias_ps, bias, aggw, aggt_ps, aggt, hid_ps, hid, y_ps, steps, stdev, xst_ps, xst, proj_ps,
         kept, stored) = (c.enter_context(nc.semaphore(n)) for n in names)
        block = c.enter_context(nc.Block())
        xt_landed = (xt0, xt1)
        stats_done = m["stats_done"]
        PER = 11
        NORMED, KV_DONE = 6, 7

        @block.sync
        def _(sp):
            for dst, src in ((w1a[:, :], m["w1"][0:FEAT, :]), (w1x[:, :], m["w1"][FEAT:2 * FEAT, :]),
                             (w1u[:, :], m["w1"][2 * FEAT:2 * FEAT + GLOB, :]), (u_c[:, :], m["u_t"]),
                             (b1_c[:, :], m["b1_t"]), (w2c[:, :, :], m["w2"].rearrange("(c p) f -> p c f", p=P)),
                             (b2b[:, :], repeat(m["b2"], 0, P)),
                             (x1[:, :, :], m["x"].rearrange("(w p) f -> p w f", p=P))):
                sp.dma_start(dst, src).then_inc(loaded, 16)

            def load_xt(k, w):
                sp.dma_start(x_tw[:, k, :], m["x_t"][:, bass.ds(w * P, P)]).then_inc(xt_landed[k], 16)

            def store_kv(w):
                sp.wait_ge(steps, PER * w + KV_DONE)
                sp.dma_start(m["kv"][0][bass.ds(w * P, P), :], kv_out[:, :]).then_inc(stored, 16)

            load_xt(0, 0)
            with sp.Fori(0, NW // 2) as pair:
                load_xt(1, 2 * pair + 1)
                store_kv(2 * pair)
                load_xt(0, 2 * pair + 2)
                store_kv(2 * pair + 1)
            store_kv(NW - 1)
            sp.wait_ge(stored, 16 * NW)

        @block.tensor
        def _(pe):
            pe.wait_ge(loaded, 16 * 8)
            for j in range(NCH):
                last = pe.matmul(bank[6][:, j:j + 1], w1u[:, j * P:(j + 1) * P], u_c[:, :], start=True, stop=True)
            last.then_inc(bias_ps, 1)

            def turn_agg(w):
                pe.wait_ge(aggw, w + 1)
                pe.transpose(bank[0][:, 0:P], agg_w[:, :], ident[:, :]).then_inc(aggt_ps, 1)

            def hidden(k, w, landings):
                pe.wait_ge(xt_landed[k], landings * 16)
                pe.wait_ge(aggt, w + 1)
                for j in range(NCH):
                    out = bank[1 + j // 4][:, j % 4 * P:(j % 4 + 1) * P]
                    pe.matmul(out, w1x[:, j * P:(j + 1) * P], x_tw[:, k, :], start=True, stop=False)
                    last = pe.matmul(out, w1a[:, j * P:(j + 1) * P], agg_t[:, :], start=False, stop=True)
                last.then_inc(hid_ps, 1)

            def outward(w):
                pe.wait_ge(hid, w + 1)
                for j in range(NCH):
                    last = pe.matmul(bank[3][:, 0:FEAT], hid_t[:, j, :], w2c[:, j, :],
                                     start=(j == 0), stop=(j == NCH - 1))
                last.then_inc(y_ps, 1)

            def project(w):
                pe.wait_ge(steps, PER * w + NORMED)
                pe.transpose(bank[4][:, 0:P], xs[:, :], ident[:, :]).then_inc(xst_ps, 1)
                pe.wait_ge(xst, w + 1)
                pe.matmul(bank[5][:, :], xs_t[:, :], m["wcat"][0][:, :], start=True, stop=True).then_inc(proj_ps, 1)

            turn_agg(0)
            hidden(0, 0, 1)

            def both(k, w, landings):
                turn_agg(w + 1)
                outward(w)
                hidden(k, w + 1, landings)
                project(w)

            with pe.Fori(0, NW // 2) as pair:
                both(1, 2 * pair, pair + 1)
                both(0, 2 * pair + 1, pair + 2)
            outward(NW - 1)
            project(NW - 1)

        @block.scalar
        def _(act):
            act.wait_ge(loaded, 16 * 8)
            act.wait_ge(bias_ps, 1)
            for j in range(NCH):
                act.activation(hbias[:, j:j + 1], bank[6][:, j:j + 1], ACT.Identity, bias=b1_c[:, j:j + 1]).then_inc(bias, 1)

            def copy_agg(w):
                act.activation(agg_w[:, :], agg_all[:, bass.ds(w, 1), :].rearrange("p a f -> p (a f)"),
                               ACT.Copy).then_inc(aggw, 1)
                act.wait_ge(aggt_ps, w + 1)
                act.activation(agg_t[:, :], bank[0][:, 0:P], ACT.Copy).then_inc(aggt, 1)

            def relu(w):
                act.wait_ge(hid_ps, w + 1)
                for j in range(NCH):
                    last = act.activation(hid_t[:, j, :], bank[1 + j // 4][:, j % 4 * P:(j % 4 + 1) * P], ACT.Relu,
                                          bias=hbias[:, j:j + 1])
                last.then_inc(hid, 1)

            def norm(w):
                act.wait_ge(steps, PER * w + 4)
                act.activation(std[:, :], mv[:, 1:2], ACT.Sqrt, bias=m["epst"][:, :]).then_inc(stdev, 1)
                act.wait_ge(steps, PER * w + NORMED)
                act.activation(x1[:, bass.ds(w, 1), :].rearrange("p a f -> p (a f)"), xs[:, :], ACT.Copy).then_inc(kept, 1)
                act.wait_ge(xst_ps, w + 1)
                act.activation(xs_t[:, :], bank[4][:, 0:P], ACT.Copy).then_inc(xst, 1)

            copy_agg(0)
            act.wait_ge(bias, NCH)
            relu(0)
            with act.Fori(0, NW - 1) as w:
                act.wait_ge(hid_ps, w + 1)
                copy_agg(w + 1)
                norm(w)
                relu(w + 1)
            norm(NW - 1)

        @block.vector
        def _(dve):
            dve.wait_ge(loaded, 16 * 8)
            with dve.Fori(0, NW) as w:
                chain = Chain(dve, steps, PER, w)
                xw = x1[:, bass.ds(w, 1), :].rearrange("p a f -> p (a f)")
                dve.wait_ge(y_ps, w + 1)
                chain(dve.tensor_tensor(res[:, :], bank[3][:, 0:FEAT], b2b[:, :], ALU.add), wait=True)
                chain(dve.tensor_tensor(res[:, :], res[:, :], xw, ALU.add), wait=True)
                chain(dve.bn_stats(stats[:, :], res[:, :]), wait=True)
                dve.sem_inc(stats_done, 1)
                chain(dve.bn_aggr(mv[:, :], stats[:, :]), wait=True)
                dve.wait_ge(stdev, w + 1)
                chain(dve.reciprocal(std[:, :], std[:, :]), wait=True)
                chain(dve.tensor_scalar(xs[:, :], res[:, :], mv[:, 0:1], std[:, 0:1], ALU.subtract, ALU.mult))
                dve.wait_ge(proj_ps, w + 1)
                dve.wait_ge(stored, 16 * w)
                store_projections(dve, chain, m, 0, w, bank[5], kv_out, prod[:, :])


def attend_stage(nc, m, layer):
    (q_all, s_all, x1, onehot, ring, bank, ident, identb, sel, ew_sb, src_sb, web) = (m[k] for k in (
        "q_all", "s_all", "x1", "onehot", "ring", "bank", "ident", "identb", "sel", "ew_sb", "src_sb", "web"))
    kv_rows = m["kv"][layer]
    last_layer = layer == 1
    LAG = 1
    CREDIT = 2 * SLOTS - 2
    with ExitStack() as c:
        def sb(name, shape, dt=F32):
            return c.enter_context(nc.sbuf_tensor(f"a{layer}_{name}", shape, dt))

        idx = sb("idx", [P, SLOTS, BODY], I32)
        onehot_t = [sb(f"onehot_t{s}", [P, HALF, P]) for s in (0, 1)]
        mask = [sb(f"mask{s}", [P, HALF, P], BF16) for s in (0, 1)]
        prod = sb("prod", [P, HALF, FEAT])
        dots = sb("dots", [P, HALF, HEADS])
        ewq = sb("ewq", [P, HALF, HEADS])
        score = [sb(f"score{s}", [P, P]) for s in (0, 1)]
        score_t = [sb(f"score_t{s}", [P, P], BF16) for s in (0, 1)]
        maxes = [sb(f"maxes{s}", [P, 1 + HALF, HEADS]) for s in (0, 1)]
        fall = sb("fall", [P, HEADS])
        decay = sb("decay", [P, HEADS])
        shifted = sb("shifted", [P, HALF, HEADS])
        pay = [sb(f"pay{s}", [P, HALF, HEADS, HP]) for s in (0, 1)]
        acc = sb("acc", [P, HEADS, HP])
        rden = sb("rden", [P, HEADS])
        msg = sb("msg", [P, HEADS, HC])
        hrow = sb("hrow", [P, FEAT])
        h_t = sb("h_t", [FEAT, P])
        kv_out = sb("kv_out", [P, 2 * FEAT])
        stats = sb("stats", [P, 6])
        mv = sb("mv", [P, 2])
        mv_all = sb("mv_all", [P, NW, 2])
        rstd = sb("rstd", [P, NW])
        landed = [c.enter_context(nc.semaphore(f"a{layer}_landed{k}")) for k in range(SLOTS)]
        (rows_ready, idx_there, begun, hot, turned_ps, turned, masked, q_ps, prodded, dotted, ewq_there, scored,
         score_ps, score_tr, spread, maxed, new_max, falls, decayed, max_ps, shifts, weighed, valued, edged, summed,
         shrunk, added, flushed, reset, ready0, steps, ht_ps, ht, proj_ps, kept, stored) = (
            c.enter_context(nc.semaphore(f"a{layer}_{n}")) for n in (
                "rows_ready", "idx_there", "begun", "hot", "turned_ps", "turned", "masked", "q_ps", "prodded",
                "dotted", "ewq_there", "scored", "score_ps", "score_tr", "spread", "maxed", "new_max", "falls",
                "decayed", "max_ps", "shifts", "weighed", "valued", "edged", "summed", "shrunk", "added", "flushed",
                "reset", "ready0", "steps", "ht_ps", "ht", "proj_ps", "kept", "stored"))
        block = c.enter_context(nc.Block())
        stats_done = m["stats_done"]
        PER = 6 + (5 if not last_layer else 4)
        NORMED, KV_DONE = 6, 7

        def q_bank(s):
            return bank[2 + s][:, 0:HALF * QW].rearrange("p (t q) -> p t q", t=HALF)

        def max_bank(s):
            return bank[4][:, 2 * P + s * HALF * HEADS:2 * P + (s + 1) * HALF * HEADS]

        @block.gpsimd
        def _(pool):
            def gather(k, i, t):
                pool.wait_ge(valued, 2 * i)
                pool.tensor_copy(idx[:, k, :], src_sb[:, bass.ds(t, BODY)]).then_inc(idx_there, 1)
                pool.wait_ge(idx_there, i + 1)
                pool.sem_inc(begun, 1)
                for n in range(BODY):
                    pool.indirect_dma_start(
                        out=ring[:, k, n, :], out_offset=None, in_=kv_rows[:, :],
                        in_offset=bass.IndirectOffsetOnAxis(ap=idx[:, k, n:n + 1], axis=0)).then_inc(landed[k], 16)

            total, one, tell = fill_ring(pool, m, NW, LAG, gather, landed, 16 * BODY, rows_ready)
            first_tile = pool.value_load(m["tab"][0:1, 1, NW:NW + 1], min_val=0, max_val=NT)
            one(total, (total, first_tile))
            tell(total + SLOTS)

        @block.vector
        def _(dve):
            def products(s, ahead, first=False):
                i, w, row = ahead
                g1 = 2 * i + s + 1
                dve.wait_ge(q_ps, g1)
                if s == 0:
                    dve.wait_ge(rows_ready, i + 1 + LAG)
                slot = bass.ds(i % SLOTS, 1)
                dve.tensor_tensor(prod[:, :, :], q_bank(s)[:, :, 0:FEAT],
                                  ring[:, slot, HALF * s:HALF * (s + 1), 0:FEAT].rearrange("p a t f -> p (a t) f"),
                                  ALU.mult).then_inc(prodded, 1)
                dve.wait_ge(prodded, g1)
                dve.tensor_reduce(dots[:, :, :].rearrange("p t h -> p (t h)"),
                                  prod[:, :, :].rearrange("p t (h c) -> p (t h) c", h=HEADS), AX.X,
                                  ALU.add).then_inc(dotted, 1)

            def scores(s, ahead):
                i, w, row = ahead
                g1 = 2 * i + s + 1
                t = m["tile_of"](i, row, dve)
                dve.tensor_tensor(ewq[:, :, :], q_bank(s)[:, :, FEAT:QW],
                                  repeat(ew_sb[:, bass.ds(t + HALF * s, HALF)].unsqueeze(2), 2, HEADS),
                                  ALU.mult).then_inc(ewq_there, 1)
                dve.wait_ge(ewq_there, g1)
                dve.wait_ge(dotted, g1)
                dve.tensor_tensor(score[s][:, 0:HALF * HEADS], dots[:, :, :].rearrange("p t h -> p (t h)"),
                                  ewq[:, :, :].rearrange("p t h -> p (t h)"), ALU.add).then_inc(scored, 1)

            def first():
                for buf, value in ((score[0][:, :], 0.0), (score[1][:, :], 0.0), (acc[:, :, :], 0.0),
                                   (bank[7][:, 0:PW], 0.0), (maxes[0][:, 0, :], -2 * BIG)):
                    dve.memset(buf, value).then_inc(ready0, 1)
                dve.wait_ge(ready0, 5)
                dve.sem_inc(valued, CREDIT)
                now = (0, 0, (0, dve.value_load(m["tab"][0:1, 1, 0:1], min_val=0, max_val=NT)))
                make_onehot(dve, m, 0, now).then_inc(hot, 1)
                products(0, now)
                scores(0, now)

            def step(s, now, ahead):
                i, w, row = now
                g = 2 * i + s
                dve.wait_ge(summed, g)
                make_onehot(dve, m, 1 - s, ahead).then_inc(hot, 1)
                dve.wait_ge(shrunk, g)
                dve.tensor_tensor(acc[:, :, :].rearrange("p h c -> p (h c)"),
                                  acc[:, :, :].rearrange("p h c -> p (h c)"), bank[7][:, 0:PW],
                                  ALU.add).then_inc(added, 1)
                for k in range(HALF):
                    dve.wait_ge(spread, HALF * g + k + 1)
                    dve.tensor_reduce(maxes[s][:, 1 + k, :],
                                      bank[5 + k][:, :].rearrange("p (h e) -> p h e", h=HEADS), AX.X,
                                      ALU.max).then_inc(maxed, 1)
                dve.wait_ge(maxed, HALF * g + HALF)
                dve.wait_ge(reset, w)
                dve.tensor_reduce(maxes[1 - s][:, 0, :], maxes[s][:, :, :].rearrange("p k h -> p h k"), AX.X,
                                  ALU.max).then_inc(new_max, 1)
                dve.wait_ge(new_max, g + 1)
                dve.tensor_tensor(fall[:, :], maxes[s][:, 0, :], maxes[1 - s][:, 0, :],
                                  ALU.subtract).then_inc(falls, 1)
                products(1 - s, ahead)
                dve.wait_ge(max_ps, g + 1)
                dve.tensor_tensor(shifted[:, :, :].rearrange("p t h -> p (t h)"), score[s][:, 0:HALF * HEADS],
                                  max_bank(s), ALU.subtract).then_inc(shifts, 1)
                scores(1 - s, ahead)
                dve.wait_ge(decayed, g + 1)
                dve.wait_ge(added, g + 1)
                dve.tensor_tensor(acc[:, :, :], acc[:, :, :], repeat(decay[:, :].unsqueeze(2), 2, HP),
                                  ALU.mult).then_inc(shrunk, 1)
                dve.wait_ge(weighed, g + 1)
                weight = pay[s][:, :, :, HC:HC + 1]
                t = m["tile_of"](i, row, dve)
                dve.tensor_tensor(pay[s][:, :, :, HC + 1:HP].rearrange("p t h a -> p t (h a)"),
                                  weight.rearrange("p t h a -> p t (h a)"),
                                  repeat(ew_sb[:, bass.ds(t + HALF * s, HALF)].unsqueeze(2), 2, HEADS),
                                  ALU.mult).then_inc(edged, 1)
                v = ring[:, bass.ds(i % SLOTS, 1), HALF * s:HALF * (s + 1), FEAT:2 * FEAT]
                dve.tensor_tensor(pay[s][:, :, :, 0:HC], v.rearrange("p a t (h c) -> p (a t) h c", h=HEADS),
                                  repeat(weight, 3, HC), ALU.mult).then_inc(valued, 1)

            def end(w, b):
                chain = Chain(dve, steps, PER, w)
                here = bass.ds(w, 1)
                flat = msg[:, :, :].rearrange("p h c -> p (h c)")
                dve.wait_ge(summed, 2 * b)
                dve.wait_ge(shrunk, 2 * b)
                dve.tensor_tensor(acc[:, :, :].rearrange("p h c -> p (h c)"),
                                  acc[:, :, :].rearrange("p h c -> p (h c)"), bank[7][:, 0:PW],
                                  ALU.add).then_inc(flushed, 1)
                dve.memset(maxes[0][:, 0, :], -2 * BIG).then_inc(reset, 1)
                dve.wait_ge(flushed, w + 1)
                chain(dve.tensor_scalar(rden[:, :].unsqueeze(2), acc[:, :, HC:HC + 1], 1e-16, None, ALU.add))
                chain(dve.tensor_tensor(msg[:, :, :], web[layer][:, :].rearrange("p (h c) -> p h c", h=HEADS),
                                        repeat(acc[:, :, HC + 1:HP], 2, HC), ALU.mult), wait=True)
                chain(dve.reciprocal(rden[:, :], rden[:, :]))
                chain(dve.tensor_tensor(msg[:, :, :], msg[:, :, :], acc[:, :, 0:HC], ALU.add), wait=True)
                chain(dve.tensor_tensor(msg[:, :, :], msg[:, :, :], repeat(rden[:, :].unsqueeze(2), 2, HC),
                                        ALU.mult), wait=True)
                chain(dve.tensor_tensor(hrow[:, :], flat, s_all[:, here, :].rearrange("p a f -> p (a f)"), ALU.add),
                      wait=True)
                if not last_layer:
                    dve.wait_ge(proj_ps, w + 1)
                    dve.wait_ge(stored, 16 * w)
                    store_projections(dve, chain, m, 1, w, bank[1], kv_out, flat)
                else:
                    xw = x1[:, here, :].rearrange("p a f -> p (a f)")
                    chain(dve.scalar_tensor_tensor(hrow[:, :], hrow[:, :], 0.0, xw, ALU.max, ALU.add), wait=True)
                    chain(dve.bn_stats(stats[:, :], hrow[:, :]), wait=True)
                    dve.sem_inc(stats_done, 1)
                    chain(dve.bn_aggr(mv[:, :], stats[:, :]), wait=True)
                    dve.wait_ge(kept, w)
                    chain(dve.tensor_copy(mv_all[:, here, :].rearrange("p a b -> p (a b)"), mv[:, :]))

            in_halves(dve, m, first, step, end)
            if last_layer:
                dve.wait_ge(kept, NW + 1)
                dve.reciprocal(rstd[:, :], rstd[:, :]).then_inc(ready0, 1)
                dve.wait_ge(ready0, 6)
                for n in range(0, NW, OUTW):
                    part = x1[:, n:n + OUTW, :]
                    dve.tensor_tensor(part, part, repeat(mv_all[:, n:n + OUTW, 0:1], 2, FEAT),
                                      ALU.subtract).then_inc(ready0, 1)
                    dve.wait_ge(ready0, 7 + 2 * (n // OUTW))
                    dve.tensor_tensor(part, part, repeat(rstd[:, n:n + OUTW].unsqueeze(2), 2, FEAT),
                                      ALU.mult).then_inc(ready0, 1)

        @block.tensor
        def _(pe):
            def turn(s, g, wait):
                pe.wait_ge(hot, g + 1)
                if wait:
                    pe.wait_ge(masked, g - 1)
                for k in range(HALF):
                    o = (s * HALF + k) * P
                    last = pe.transpose(bank[0][:, o:o + P], onehot[s][:, k, :], ident[:, :])
                last.then_inc(turned_ps, 1)

            def fetch_q(s, g, w, wait):
                pe.wait_ge(turned, g + 1)
                if wait:
                    pe.wait_ge(scored, g - 1)
                q = q_all[:, bass.ds(w, 1), :].rearrange("p a q -> p (a q)")
                for k in range(HALF):
                    last = pe.matmul(q_bank(s)[:, k, :], onehot_t[s][:, k, :], q, start=True, stop=True)
                last.then_inc(q_ps, 1)

            def turn_scores(s, g, wait):
                pe.wait_ge(scored, g + 1)
                if wait:
                    pe.wait_ge(score_tr, g - 1)
                pe.transpose(bank[4][:, s * P:(s + 1) * P], score[s][:, :], ident[:, :]).then_inc(score_ps, 1)

            def first():
                turn(0, 0, False)
                fetch_q(0, 0, 0, False)
                turn_scores(0, 0, False)

            def step(s, now, ahead):
                i, w, _ = now
                g = 2 * i + s
                pe.wait_ge(masked, g + 1)
                pe.wait_ge(score_tr, g + 1)
                pe.wait_ge(new_max, g)
                for k in range(HALF):
                    pe.matmul(bank[5 + k][:, :], identb[:, :], repeat(mask[s][:, k, :].unsqueeze(1), 1, HEADS),
                              start=True, stop=False)
                    for h in range(HEADS):
                        last = pe.matmul(bank[5 + k][:, h * P:(h + 1) * P], sel[:, k * HEADS + h, :],
                                         score_t[s][:, :], start=False, stop=(h == HEADS - 1))
                    last.then_inc(spread, 1)
                turn(1 - s, g + 1, True)
                fetch_q(1 - s, g + 1, ahead[1], True)
                pe.wait_ge(new_max, g + 1)
                for k in range(HALF):
                    last = pe.matmul(max_bank(s)[:, k * HEADS:(k + 1) * HEADS], onehot_t[s][:, k, :],
                                     maxes[1 - s][:, 0, :], start=True, stop=True)
                last.then_inc(max_ps, 1)
                turn_scores(1 - s, g + 1, True)
                pe.wait_ge(valued, CREDIT + g + 1)
                pe.wait_ge(edged, g + 1)
                pe.wait_ge(added, g + 1)
                for k in range(HALF):
                    last = pe.matmul(bank[7][:, 0:PW], onehot[s][:, k, :],
                                     pay[s][:, k, :, :].rearrange("p h c -> p (h c)"),
                                     start=(k == 0), stop=(k == HALF - 1))
                last.then_inc(summed, 1)

            def end(w, b):
                if last_layer:
                    return
                pe.wait_ge(steps, PER * w + NORMED)
                pe.transpose(bank[1][:, 0:P], hrow[:, :], ident[:, :]).then_inc(ht_ps, 1)
                pe.wait_ge(ht, w + 1)
                pe.matmul(bank[1][:, :], h_t[:, :], m["wcat"][1][:, :], start=True, stop=True).then_inc(proj_ps, 1)

            in_halves(pe, m, first, step, end)

        @block.scalar
        def _(act):
            def copy_turned(s, g, wait):
                act.wait_ge(turned_ps, g + 1)
                if wait:
                    act.wait_ge(max_ps, g - 1)
                here = bank[0][:, s * HALF * P:(s + 1) * HALF * P]
                act.activation(onehot_t[s][:, :, :].rearrange("p t e -> p (t e)"), here, ACT.Copy).then_inc(turned, 1)
                act.activation(mask[s][:, :, :].rearrange("p t e -> p (t e)"), here, ACT.Copy, scale=BIG,
                               bias=-BIG).then_inc(masked, 1)

            def copy_scores(s, g):
                act.wait_ge(score_ps, g + 1)
                act.activation(score_t[s][:, :], bank[4][:, s * P:(s + 1) * P], ACT.Copy).then_inc(score_tr, 1)

            def first():
                copy_turned(0, 0, False)
                copy_scores(0, 0)

            def step(s, now, ahead):
                i, w, _ = now
                g = 2 * i + s
                copy_turned(1 - s, g + 1, True)
                act.wait_ge(falls, g + 1)
                act.wait_ge(shrunk, g)
                act.activation(decay[:, :], fall[:, :], ACT.Exp).then_inc(decayed, 1)
                act.wait_ge(shifts, g + 1)
                act.activation(pay[s][:, :, :, HC:HC + 1].rearrange("p t h a -> p t (h a)"), shifted[:, :, :],
                               ACT.Exp).then_inc(weighed, 1)
                copy_scores(1 - s, g + 1)

            def end(w, b):
                if last_layer:
                    act.wait_ge(steps, PER * w + 7)
                    act.activation(x1[:, bass.ds(w, 1), :].rearrange("p a f -> p (a f)"), hrow[:, :],
                                   ACT.Copy).then_inc(kept, 1)
                else:
                    act.wait_ge(ht_ps, w + 1)
                    act.activation(h_t[:, :], bank[1][:, 0:P], ACT.Relu).then_inc(ht, 1)

            in_halves(act, m, first, step, end)
            if last_layer:
                act.wait_ge(steps, PER * NW)
                act.activation(rstd[:, :], mv_all[:, :, 1:2].rearrange("p w a -> p (w a)"), ACT.Sqrt,
                               bias=m["epst"][:, :]).then_inc(kept, 1)

        @block.sync
        def _(sp):
            if not last_layer:
                with sp.Fori(0, NW) as w:
                    sp.wait_ge(steps, PER * w + KV_DONE)
                    sp.dma_start(m["kv"][1][bass.ds(w * P, P), :], kv_out[:, :]).then_inc(stored, 16)
                sp.wait_ge(stored, 16 * NW)
            else:
                out_rows = m["out"].rearrange("(w p) f -> p w f", p=P)
                for n in range(0, NW, OUTW):
                    sp.wait_ge(ready0, 8 + 2 * (n // OUTW))
                    sp.dma_start(out_rows[:, n:n + OUTW, :], x1[:, n:n + OUTW, :]).then_inc(stored, 16)
                sp.wait_ge(stored, 16 * (NW // OUTW))


_SHAPES = ("x", "x_t", "src_t", "dst_t", "dst_r", "ew_t", "edge_attr", "u_t", "w1", "b1_t", "w2", "b2",
           "wcat1", "bcat1", "we1", "wcat2", "bcat2", "we2")


def kernel(**inp):
    import concourse.bacc as bacc
    from concourse.bass_utils import run_bass_kernel_spmd

    a = {k: np.asarray(v) for k, v in inp.items()}

    def rows(v, n):
        return np.concatenate([v, np.zeros((n - v.shape[0],) + v.shape[1:], v.dtype)])

    def by_tile(v, fill):
        v = np.concatenate([v, np.full(TABLE * P - v.shape[0], fill, v.dtype)])
        return np.ascontiguousarray(v.reshape(TABLE, P).T)

    arrays = {
        "x": rows(a["x"], ROWS),
        "x_t": np.ascontiguousarray(rows(a["x"], ROWS).T),
        "src_t": by_tile(a["src"], 0),
        "dst_t": by_tile(a["dst"], -1),
        "dst_r": np.pad(a["dst"], (0, NT * P - EDGES), mode="edge").reshape(NT, P),
        "ew_t": by_tile(a["edge_weight"], 0),
        "edge_attr": rows(a["edge_attr_128"], TABLE * P),
        "u_t": a["L0_gnn_u"].reshape(GLOB, 1),
        "w1": a["L0_gnn_W1"],
        "b1_t": np.ascontiguousarray(a["L0_gnn_b1"].reshape(NCH, P).T),
        "w2": a["L0_gnn_W2"],
        "b2": a["L0_gnn_b2"].reshape(1, FEAT),
    }
    for n in ("1", "2"):
        w = [a[f"L1_gnn_W{k}{n}"] for k in "qkvs"]
        b = [a[f"L1_gnn_b{k}{n}"] for k in "qkvs"]
        arrays["wcat" + n] = np.concatenate(w, axis=1)
        arrays["bcat" + n] = np.concatenate(b).reshape(1, 4 * FEAT)
        arrays["we" + n] = a["L1_gnn_We" + n].reshape(1, FEAT)

    nc = bacc.Bacc("TRN2", target_bir_lowering=False, num_devices=1)
    args = [nc.dram_tensor(f"in_{k}", arrays[k].shape, mybir.dt.from_np(arrays[k].dtype), kind="ExternalInput").ap()
            for k in _SHAPES]
    out = nc.dram_tensor("out_0", (ROWS, FEAT), F32, kind="ExternalOutput").ap()
    build(nc, *args, out)
    r = run_bass_kernel_spmd(nc, [{f"in_{k}": arrays[k] for k in _SHAPES}], core_ids=[0])
    return r.results[0]["out_0"][:NODES]
```

```python
from contextlib import ExitStack

import concourse.bass as bass
import concourse.mybir as mybir
import numpy as np

F32 = mybir.dt.float32
BF16 = mybir.dt.bfloat16
I32 = mybir.dt.int32
ALU = mybir.AluOpType
ACT = mybir.ActivationFunctionType
AX = mybir.AxisListType

P = 128
NODES, EDGES, FEAT, HEADS = 6250, 100000, 128, 4
HC = FEAT // HEADS
GLOB, HID = 16, 1024
NW = -(-NODES // P)
ROWS = NW * P
NT = -(-EDGES // P)
BODY = 4
HALF = BODY // 2
MIN_BODIES = 2
TABLE = NT + MIN_BODIES * BODY + 2
TB = -(-NT // P)
NCH = HID // P
SLOTS = 4
QW = FEAT + HEADS
HP = HC + 2
PW = HEADS * HP
OUTW = 7
OUT_OF = (-(-OUTW // 2), OUTW // 2)
BIG = float(2 ** 100)
SCALE = float(HC) ** -0.5
EPS = 1e-5
PACK = 1024
SUM_OF_COUNTS = "the bounds stage makes them so"
MAXB = NW * (-(-(NT + 1) // BODY)) + NW * MIN_BODIES


def repeat(ap, axis, n):
    shape = list(ap.shape)
    shape[axis] = n
    return ap.broadcast_to(shape)


def build(nc, x, x_t, src_t, dst_t, dst_r, ew_t, edge_attr, u_t, w1, b1_t, w2, b2,
          wcat1, bcat1, we1, wcat2, bcat2, we2, out):
    kv = [nc.dram_tensor(f"kv{n}", [ROWS, 2 * FEAT], F32).ap() for n in (1, 2)]
    ctx = ExitStack()
    with ctx:
        def sb(name, shape, dt=F32):
            return ctx.enter_context(nc.sbuf_tensor(name, shape, dt))

        def pb(name, shape, dt=F32):
            return ctx.enter_context(nc.psum_tensor(name, shape, dt))

        def sem(name):
            return ctx.enter_context(nc.semaphore(name))

        src_sb = sb("src_sb", [P, TABLE], I32)
        dst_sb = sb("dst_sb", [P, TABLE])
        ew_sb = sb("ew_sb", [P, TABLE])
        dst_i = sb("dst_i", [P, TABLE], I32)
        tab = sb("tab", [1, 2, NW + 2], I32)
        wbase = sb("wbase", [P, NW + 1])
        iota_n = sb("iota_n", [P, P])
        ident = sb("ident", [P, P])
        identb = sb("identb", [P, P], BF16)
        ones = sb("ones", [P, P])
        sel = sb("sel", [P, 2 * HEADS, P], BF16)
        q_all = sb("q_all", [P, NW + 1, QW])
        s_all = sb("s_all", [P, NW + 1, FEAT])
        x1 = sb("x1", [P, NW, FEAT])
        acc_all = sb("acc_all", [P, NW + 1, PW])
        agg_all = acc_all[:, 1:NW + 1, 0:FEAT]
        wcat = [sb(f"wcat{n}", [P, 4 * FEAT]) for n in (0, 1)]
        bcat = [sb(f"bcat{n}", [P, 4 * FEAT]) for n in (0, 1)]
        web = [sb(f"web{n}", [P, FEAT]) for n in (0, 1)]
        zerob = sb("zerob", [P, P], BF16)
        ring = sb("ring", [P, SLOTS, BODY, 2 * FEAT])
        epst = sb("epst", [P, 1])

        stats_done = sem("stats_done")

        bank = [pb(f"bank{n}", [P, 512]) for n in range(8)]

        def tile_of(i, w_row, eng):
            first_body, first_tile = w_row
            return nc.s_assert_within(
                first_tile + (i - first_body) * BODY, 0, TABLE - BODY,
                skip_runtime_bounds_check_because="the bodies of a window end at most two bodies past its last tile")

        def window(eng, w):
            return unpack(eng, 0, w)

        def after(eng, w):
            return unpack(eng, 1, w)

        def unpack(eng, row, w):
            both = eng.value_load(tab[0:1, row, bass.ds(w, 1)], min_val=0, max_val=PACK * MAXB + NT)
            a = nc.s_assert_within(eng.snap(both // PACK), 0, MAXB, skip_runtime_bounds_check_because=SUM_OF_COUNTS)
            t = nc.s_assert_within(eng.snap(both % PACK), 0, NT, skip_runtime_bounds_check_because=SUM_OF_COUNTS)
            return a, t

        bounds_stage(nc, ctx, locals())
        collect_stage(nc, locals())
        update_stage(nc, locals())
        attend_stage(nc, locals(), 0)
        project_stage(nc, locals())
        attend_stage(nc, locals(), 1)
        output_stage(nc, locals())


def bounds_stage(nc, ctx, m):
    (src_sb, dst_sb, dst_i, ew_sb, tab, wbase, iota_n, ident, identb, ones, sel, q_all, x1, wcat, bcat,
     web, bank, s_all, epst) = (m[k] for k in (
        "src_sb", "dst_sb", "dst_i", "ew_sb", "tab", "wbase", "iota_n", "ident", "identb", "ones", "sel",
        "q_all", "x1", "wcat", "bcat", "web", "bank", "s_all", "epst"))
    W1 = NW + 1
    FAR = 1024.0
    with ExitStack() as c:
        def sb(name, shape, dt=F32):
            return c.enter_context(nc.sbuf_tensor(name, shape, dt))

        dst_rows = sb("dst_rows", [P, TB, P], I32)
        low = sb("low", [P, TB])
        high = sb("high", [P, TB])
        tile_no = sb("tile_no", [P, TB])
        wrow = sb("wrow", [P, W1])
        wend = sb("wend", [P, W1])
        below = sb("below", [P, TB, W1])
        above = sb("above", [P, TB, W1])
        reach = sb("reach", [P, 2, W1])
        reach_c = sb("reach_c", [2 * W1, 1])
        row = sb("row", [1, 2 * W1])
        first = sb("first", [1, W1 + 1])
        count = sb("count", [1, W1])
        count_i = sb("count_i", [1, W1], I32)
        zrow = sb("zrow", [1, W1])
        cum = sb("cum", [1, W1 + 1])
        loaded = c.enter_context(nc.semaphore("b_loaded"))
        made = c.enter_context(nc.semaphore("b_made"))
        steps = c.enter_context(nc.semaphore("b_steps"))
        turned = c.enter_context(nc.semaphore("b_turned"))
        block = c.enter_context(nc.Block())
        blank = [0]

        @block.gpsimd
        def _(pool):
            pool.iota(iota_n[:, :], [[1, P]], base=0, channel_multiplier=0,
                      allow_small_or_imprecise_dtypes=True).then_inc(made, 1)
            pool.iota(wbase[:, :], [[P, W1]], base=0, channel_multiplier=0,
                      allow_small_or_imprecise_dtypes=True).then_inc(made, 1)
            pool.iota(tile_no[:, :], [[P, TB]], base=0, channel_multiplier=1,
                      allow_small_or_imprecise_dtypes=True).then_inc(made, 1)
            pool.memset(ones[:, :], 1.0).then_inc(made, 1)
            pool.memset(sel[:, :, :], 0.0).then_inc(made, 1)
            pool.wait_ge(made, 5)
            pool.affine_select(out=ident[:, :], in_=ones[:, :], compare_op=ALU.is_equal, fill=0.0,
                               base=0, pattern=[[-1, P]], channel_multiplier=1).then_inc(made, 1)
            pool.affine_select(out=sel[:, :, :], in_=sel[:, :, :], compare_op=ALU.not_equal, fill=1.0,
                               base=0, pattern=[[-1, 2 * HEADS], [0, P]], channel_multiplier=1).then_inc(made, 1)
            pool.wait_ge(made, 7)
            pool.tensor_copy(identb[:, :], ident[:, :]).then_inc(made, 1)
            pool.memset(q_all[:, NW, :], 0.0).then_inc(made, 1)
            pool.memset(epst[:, :], EPS).then_inc(made, 1)
            pool.memset(m["zerob"][:, :], 0.0).then_inc(made, 1)
            pool.wait_ge(made, 11)

        @block.sync
        def _(sp):
            sp.dma_start(dst_i[:, :], m["dst_t"]).then_inc(loaded, 16)
            sp.wait_ge(steps, 1)
            full = NT // P * P
            sp.dma_start(dst_rows[:, 0:NT // P, :],
                         m["dst_r"][0:full, :].rearrange("(b p) e -> p b e", p=P)).then_inc(loaded, 16)
            sp.dma_start(dst_rows[0:NT - full, NT // P, :], m["dst_r"][full:NT, :]).then_inc(loaded, 16)
            sp.dma_start(src_sb[:, :], m["src_t"]).then_inc(loaded, 16)
            sp.dma_start(ew_sb[:, :], m["ew_t"]).then_inc(loaded, 16)
            for n, (wc, bc, we) in enumerate((("wcat1", "bcat1", "we1"), ("wcat2", "bcat2", "we2"))):
                sp.dma_start(wcat[n][:, :], m[wc]).then_inc(loaded, 16)
                sp.dma_start(bcat[n][:, :], repeat(m[bc], 0, P)).then_inc(loaded, 16)
                sp.dma_start(web[n][:, :], repeat(m[we], 0, P)).then_inc(loaded, 16)
            sp.wait_ge(loaded, 16 * 11)

        @block.vector
        def _(dve):
            n = [0]

            def step(ins):
                n[0] += 1
                ins.then_inc(steps, 1)
                dve.wait_ge(steps, n[0])

            step(dve.memset(dst_rows[:, :, :], 1 << 20))
            dve.wait_ge(loaded, 16 * 11)
            dve.wait_ge(made, 11)
            step(dve.tensor_copy(dst_sb[:, :], dst_i[:, :]))
            for b in bcat:
                step(dve.tensor_scalar(b[:, 0:FEAT], b[:, 0:FEAT], SCALE, None, ALU.mult))
            step(dve.tensor_reduce(low[:, :], dst_rows[:, :, :], AX.X, ALU.min))
            step(dve.tensor_reduce(high[:, :], dst_rows[:, :, :], AX.X, ALU.max))
            step(dve.tensor_scalar(wend[:, :], wbase[:, :], float(P), None, ALU.add))
            low_b = repeat(low[:, :].unsqueeze(2), 2, W1)
            high_b = repeat(high[:, :].unsqueeze(2), 2, W1)
            step(dve.tensor_tensor(below[:, :, :], repeat(wend[:, :].unsqueeze(1), 1, TB), low_b, ALU.is_gt))
            step(dve.tensor_tensor(above[:, :, :], repeat(wbase[:, :].unsqueeze(1), 1, TB), high_b, ALU.is_le))
            step(dve.tensor_tensor(below[:, :, :], below[:, :, :], above[:, :, :], ALU.mult))
            step(dve.tensor_scalar(high[:, :], tile_no[:, :], -1.0, FAR, ALU.mult, ALU.add))
            step(dve.tensor_scalar(low[:, :], tile_no[:, :], 1.0, None, ALU.add))
            step(dve.tensor_tensor(above[:, :, :], below[:, :, :], high_b, ALU.mult))
            step(dve.tensor_tensor(below[:, :, :], below[:, :, :], low_b, ALU.mult))
            step(dve.tensor_reduce(reach[:, 0, :], below[:, :, :].rearrange("p b w -> p w b"), AX.X, ALU.max))
            step(dve.tensor_reduce(reach[:, 1, :], above[:, :, :].rearrange("p b w -> p w b"), AX.X, ALU.max))
            dve.wait_ge(turned, 1)
            step(dve.tensor_reduce(reach_c[:, :], bank[0][0:2 * W1, 0:P], AX.X, ALU.max))
            blank[0] = n[0]
            dve.wait_ge(turned, 2)
            step(dve.tensor_copy(row[:, :], bank[1][0:1, 0:2 * W1]))
            step(dve.tensor_scalar(first[:, 0:W1], row[:, W1:2 * W1], -1.0, FAR, ALU.mult, ALU.add))
            step(dve.tensor_scalar(first[:, 0:W1], first[:, 0:W1], float(NT - 1), None, ALU.min))
            step(dve.tensor_tensor(count[:, :], row[:, 0:W1], first[:, 0:W1], ALU.subtract))
            step(dve.tensor_scalar(count[:, :], count[:, :], float(BODY - 1), float(MIN_BODIES * BODY),
                                   ALU.add, ALU.max))
            step(dve.tensor_copy(count_i[:, :], count[:, :]))
            step(dve.tensor_scalar(count_i[:, :], count_i[:, :], BODY.bit_length() - 1, None,
                                   ALU.arith_shift_right))
            step(dve.tensor_copy(count[:, :], count_i[:, :]))
            step(dve.memset(zrow[:, :], 0.0))
            step(dve.memset(cum[:, 0:1], 0.0))
            step(dve.tensor_tensor_scan(cum[:, 1:W1 + 1], zrow[:, :], count[:, :], 0.0, ALU.add, ALU.add))
            step(dve.memset(first[:, W1:W1 + 1], 0.0))
            step(dve.tensor_scalar(cum[:, :], cum[:, :], float(PACK), None, ALU.mult))
            step(dve.tensor_tensor(tab[0:1, 0, 0:W1 + 1], cum[:, :], first[:, :], ALU.add))
            step(dve.scalar_tensor_tensor(tab[0:1, 1, 0:W1], cum[:, 1:W1 + 1], -float(PACK), first[:, 1:W1 + 1],
                                          ALU.add, ALU.add))

        @block.tensor
        def _(pe):
            pe.wait_ge(made, 11)
            pe.wait_ge(steps, blank[0] - 1)
            pe.transpose(bank[0][0:2 * W1, 0:P], reach[:, :, :].rearrange("p a w -> p (a w)"),
                         ident[:, :]).then_inc(turned, 1)
            pe.wait_ge(steps, blank[0])
            pe.matmul(bank[1][0:1, 0:2 * W1], reach_c[:, :], ident[0:2 * W1, 0:2 * W1],
                      start=True, stop=True).then_inc(turned, 1)


def branch4(eng, i, emit):
    k = eng.snap(i % SLOTS)
    with eng.If(k < 2):
        with eng.If(k < 1):
            emit(0)
        with eng.Else():
            emit(1)
    with eng.Else():
        with eng.If(k < 3):
            emit(2)
        with eng.Else():
            emit(3)


def fill_ring(eng, m, windows, lag, start, landed, per_body, ready):
    window, tile_of = m["window"], m["tile_of"]

    def one(i, row):
        t = eng.snap(tile_of(i, row, eng))

        def slot(k):
            start(k, i, t)
            eng.wait_ge(landed[(k - lag) % SLOTS], ((i + SLOTS - lag) // SLOTS) * per_body)
            eng.sem_inc(ready, 1)
        branch4(eng, i, slot)

    def tell(at):
        def wait(k):
            eng.wait_ge(landed[k], (at // SLOTS) * per_body)
            eng.sem_inc(ready, 1)
        branch4(eng, at, wait)

    with eng.Fori(0, windows) as w:
        a, t0 = window(eng, w)
        b, t1 = window(eng, w + 1)
        with eng.Fori(a, b) as i:
            one(i, (a, t0))
    total, first_tile = window(eng, windows)
    return total, first_tile, one, tell


def in_halves(eng, m, first, step, end):
    window = m["window"]
    first((0, 0, (0, window(eng, 0)[1])))
    with eng.Fori(0, NW) as w:
        a, t0 = window(eng, w)
        last, t1 = m["after"](eng, w)
        b = last + 1
        row = (a, t0)
        end(w, 2 * a)
        with eng.Fori(a, last) as i:
            step(0, (i, w, row), (i, w, row), (i + 1, w, row))
            step(1, (i, w, row), (i + 1, w, row), (i + 1, w, row))
        i = last
        ahead = (b, w + 1, (b, t1))
        step(0, (i, w, row), (i, w, row), ahead)
        step(1, (i, w, row), ahead, ahead)
    end(NW, 2 * window(eng, NW)[0])


def make_onehot(dve, m, out, s, now):
    i, w, row = now
    t = m["tile_of"](i, row, dve)
    return dve.scalar_tensor_tensor(
        out[:, :, :], repeat(m["iota_n"][:, :].unsqueeze(1), 1, HALF), m["wbase"][:, bass.ds(w, 1)],
        repeat(m["dst_sb"][:, bass.ds(t + HALF * s, HALF)].unsqueeze(2), 2, P), ALU.add, ALU.is_equal)


def collect_stage(nc, m):
    agg_all, ring, bank = (m[k] for k in ("agg_all", "ring", "bank"))
    edge_rows = m["edge_attr"].rearrange("(t p) f -> p t f", p=P)
    LAG = 2
    with ExitStack() as c:
        onehot = [c.enter_context(nc.sbuf_tensor(f"c_onehot{s}", [P, HALF, P], F32)) for s in (0, 1)]
        landed = [c.enter_context(nc.semaphore(f"c_landed{k}")) for k in range(SLOTS)]
        rows_ready, freed, hot, summed, closed, kept = (
            c.enter_context(nc.semaphore(n)) for n in
            ("c_rows_ready", "c_freed", "c_hot", "c_summed", "c_closed", "c_kept"))
        block = c.enter_context(nc.Block())

        @block.sync
        def _(sp):
            def load(k, i, t):
                sp.wait_ge(freed, i + 1)
                sp.dma_start(ring[:, k, :, 0:FEAT], edge_rows[:, bass.ds(t, BODY), :]).then_inc(landed[k], 16)

            sp.sem_inc(freed, SLOTS)
            total, _, _, tell = fill_ring(sp, m, NW, LAG, load, landed, 16, rows_ready)
            for back in range(LAG, 0, -1):
                tell(total + SLOTS - back)

        @block.vector
        def _(dve):
            def first(now):
                for s in (0, 1):
                    make_onehot(dve, m, onehot[s], s, now).then_inc(hot, 1)

            def step(s, now, near, far):
                dve.wait_ge(summed, 2 * now[0] + s + 1)
                make_onehot(dve, m, onehot[s], s, far).then_inc(hot, 1)
                if s == 1:
                    dve.sem_inc(freed, 1)

            def end(w, halves):
                dve.wait_ge(closed, w + 1)
                dve.tensor_copy(m["acc_all"][:, bass.ds(w, 1), 0:FEAT].rearrange("p a f -> p (a f)"),
                                bank[0][:, 0:FEAT]).then_inc(kept, 1)

            in_halves(dve, m, first, step, end)

        @block.tensor
        def _(pe):
            def zero(start):
                return pe.matmul(bank[0][:, 0:FEAT], m["zerob"][:, :], m["zerob"][:, :], start=start, stop=not start,
                                 skip_group_check=True)

            zero(True)
            zero(False).then_inc(closed, 1)
            with pe.Fori(0, NW) as w:
                a, _ = m["window"](pe, w)
                b, _ = m["window"](pe, w + 1)
                pe.wait_ge(kept, w + 1)
                zero(True)
                with pe.Fori(a, b) as i:
                    for s in (0, 1):
                        if s == 0:
                            pe.wait_ge(rows_ready, i + 1 + LAG)
                        pe.wait_ge(hot, 2 * i + s + 1)
                        for k in range(HALF):
                            rows = ring[:, bass.ds(i % SLOTS, 1), HALF * s + k, 0:FEAT].rearrange("p a f -> p (a f)")
                            last = pe.matmul(bank[0][:, 0:FEAT], onehot[s][:, k, :], rows,
                                             start=False, stop=False, skip_group_check=True)
                        last.then_inc(summed, 1)
                zero(False).then_inc(closed, 1)


def store_projections(dve, chain, m, layer, w, proj, kv_out, prod):
    q_all, s_all, bcat, web = m["q_all"], m["s_all"], m["bcat"][layer], m["web"][layer]
    here = bass.ds(w, 1)
    chain(dve.tensor_tensor(kv_out[:, :], proj[:, FEAT:3 * FEAT], bcat[:, FEAT:3 * FEAT], ALU.add))
    chain(dve.scalar_tensor_tensor(q_all[:, here, 0:FEAT].rearrange("p a f -> p (a f)"), proj[:, 0:FEAT], SCALE,
                                   bcat[:, 0:FEAT], ALU.mult, ALU.add), wait=True)
    chain(dve.tensor_tensor(s_all[:, here, :].rearrange("p a f -> p (a f)"), proj[:, 3 * FEAT:4 * FEAT],
                            bcat[:, 3 * FEAT:4 * FEAT], ALU.add))
    chain(dve.tensor_tensor(prod, q_all[:, here, 0:FEAT].rearrange("p a f -> p (a f)"), web[:, :], ALU.mult), wait=True)
    chain(dve.tensor_reduce(q_all[:, here, FEAT:QW].rearrange("p a h -> p (a h)"),
                            prod.rearrange("p (h c) -> p h c", h=HEADS), AX.X, ALU.add), wait=True)


class Chain:

    def __init__(self, eng, sem, per, turn):
        self.eng, self.sem, self.base, self.n, self.per = eng, sem, turn * per, 0, per

    def __call__(self, ins, wait=False):
        ins.then_inc(self.sem, 1)
        self.n += 1
        if wait:
            self.eng.wait_ge(self.sem, self.base + self.n)


def update_stage(nc, m):
    agg_all, x1, bank, ident = (m[k] for k in ("agg_all", "x1", "bank", "ident"))
    with ExitStack() as c:
        def sb(name, shape, dt=F32):
            return c.enter_context(nc.sbuf_tensor(name, shape, dt))

        w1a = sb("w1a", [FEAT, HID])
        w1x = sb("w1x", [FEAT, HID])
        w1u = sb("w1u", [GLOB, HID])
        u_c = sb("u_c", [GLOB, 1])
        b1_c = sb("b1_c", [P, NCH])
        hbias = sb("hbias", [P, NCH])
        w2c = sb("w2c", [P, NCH, FEAT])
        b2b = sb("b2b", [P, FEAT])
        x_tw = sb("x_tw", [FEAT, 2, P])
        agg_w = sb("agg_w", [P, FEAT])
        agg_t = sb("agg_t", [FEAT, P])
        hid_t = sb("hid_t", [P, NCH, P])
        res = sb("res", [P, FEAT])
        stats = sb("stats", [P, 6])
        mv = sb("mv", [P, 2])
        std = sb("std", [P, 1])
        xs = sb("xs", [P, FEAT])
        xs_t = sb("xs_t", [FEAT, P])
        kv_out = sb("kv_out", [P, 2 * FEAT])
        prod = sb("u_prod", [P, FEAT])
        names = ("u_loaded", "u_xt0", "u_xt1", "u_bias_ps", "u_bias", "u_aggw", "u_aggt_ps", "u_aggt", "u_hid_ps",
                 "u_hid", "u_y", "u_dve", "u_std", "u_xst_ps", "u_xst", "u_proj", "u_kept", "u_stored")
        (loaded, xt0, xt1, bias_ps, bias, aggw, aggt_ps, aggt, hid_ps, hid, y_ps, steps, stdev, xst_ps, xst, proj_ps,
         kept, stored) = (c.enter_context(nc.semaphore(n)) for n in names)
        block = c.enter_context(nc.Block())
        xt_landed = (xt0, xt1)
        stats_done = m["stats_done"]
        PER = 11
        NORMED, KV_DONE = 6, 7

        @block.sync
        def _(sp):
            for dst, src in ((w1a[:, :], m["w1"][0:FEAT, :]), (w1x[:, :], m["w1"][FEAT:2 * FEAT, :]),
                             (w1u[:, :], m["w1"][2 * FEAT:2 * FEAT + GLOB, :]), (u_c[:, :], m["u_t"]),
                             (b1_c[:, :], m["b1_t"]), (w2c[:, :, :], m["w2"].rearrange("(c p) f -> p c f", p=P)),
                             (b2b[:, :], repeat(m["b2"], 0, P)),
                             (x1[:, :, :], m["x"].rearrange("(w p) f -> p w f", p=P))):
                sp.dma_start(dst, src).then_inc(loaded, 16)

            def load_xt(k, w):
                sp.dma_start(x_tw[:, k, :], m["x_t"][:, bass.ds(w * P, P)]).then_inc(xt_landed[k], 16)

            def store_kv(w):
                sp.wait_ge(steps, PER * w + KV_DONE)
                sp.dma_start(m["kv"][0][bass.ds(w * P, P), :], kv_out[:, :]).then_inc(stored, 16)

            load_xt(0, 0)
            with sp.Fori(0, NW // 2) as pair:
                load_xt(1, 2 * pair + 1)
                store_kv(2 * pair)
                load_xt(0, 2 * pair + 2)
                store_kv(2 * pair + 1)
            store_kv(NW - 1)
            sp.wait_ge(stored, 16 * NW)

        @block.tensor
        def _(pe):
            pe.wait_ge(loaded, 16 * 8)
            for j in range(NCH):
                last = pe.matmul(bank[6][:, j:j + 1], w1u[:, j * P:(j + 1) * P], u_c[:, :], start=True, stop=True)
            last.then_inc(bias_ps, 1)

            def turn_agg(w):
                pe.wait_ge(aggw, w + 1)
                pe.transpose(bank[0][:, 0:P], agg_w[:, :], ident[:, :]).then_inc(aggt_ps, 1)

            def hidden(k, w, landings):
                pe.wait_ge(xt_landed[k], landings * 16)
                pe.wait_ge(aggt, w + 1)
                for j in range(NCH):
                    out = bank[1 + j // 4][:, j % 4 * P:(j % 4 + 1) * P]
                    pe.matmul(out, w1x[:, j * P:(j + 1) * P], x_tw[:, k, :], start=True, stop=False)
                    last = pe.matmul(out, w1a[:, j * P:(j + 1) * P], agg_t[:, :], start=False, stop=True)
                last.then_inc(hid_ps, 1)

            def outward(w):
                pe.wait_ge(hid, w + 1)
                for j in range(NCH):
                    last = pe.matmul(bank[3][:, 0:FEAT], hid_t[:, j, :], w2c[:, j, :],
                                     start=(j == 0), stop=(j == NCH - 1))
                last.then_inc(y_ps, 1)

            def project(w):
                pe.wait_ge(steps, PER * w + NORMED)
                pe.transpose(bank[4][:, 0:P], xs[:, :], ident[:, :]).then_inc(xst_ps, 1)
                pe.wait_ge(xst, w + 1)
                pe.matmul(bank[5][:, :], xs_t[:, :], m["wcat"][0][:, :], start=True, stop=True).then_inc(proj_ps, 1)

            turn_agg(0)
            hidden(0, 0, 1)

            def both(k, w, landings):
                turn_agg(w + 1)
                outward(w)
                hidden(k, w + 1, landings)
                project(w)

            with pe.Fori(0, NW // 2) as pair:
                both(1, 2 * pair, pair + 1)
                both(0, 2 * pair + 1, pair + 2)
            outward(NW - 1)
            project(NW - 1)

        @block.scalar
        def _(act):
            act.wait_ge(loaded, 16 * 8)
            act.wait_ge(bias_ps, 1)
            for j in range(NCH):
                act.activation(hbias[:, j:j + 1], bank[6][:, j:j + 1], ACT.Identity, bias=b1_c[:, j:j + 1]).then_inc(bias, 1)

            def copy_agg(w):
                act.activation(agg_w[:, :], agg_all[:, bass.ds(w, 1), :].rearrange("p a f -> p (a f)"),
                               ACT.Copy).then_inc(aggw, 1)
                act.wait_ge(aggt_ps, w + 1)
                act.activation(agg_t[:, :], bank[0][:, 0:P], ACT.Copy).then_inc(aggt, 1)

            def relu(w):
                act.wait_ge(hid_ps, w + 1)
                for j in range(NCH):
                    last = act.activation(hid_t[:, j, :], bank[1 + j // 4][:, j % 4 * P:(j % 4 + 1) * P], ACT.Relu,
                                          bias=hbias[:, j:j + 1])
                last.then_inc(hid, 1)

            def norm(w):
                act.wait_ge(steps, PER * w + 4)
                act.activation(std[:, :], mv[:, 1:2], ACT.Sqrt, bias=m["epst"][:, :]).then_inc(stdev, 1)
                act.wait_ge(steps, PER * w + NORMED)
                act.activation(x1[:, bass.ds(w, 1), :].rearrange("p a f -> p (a f)"), xs[:, :], ACT.Copy).then_inc(kept, 1)
                act.wait_ge(xst_ps, w + 1)
                act.activation(xs_t[:, :], bank[4][:, 0:P], ACT.Copy).then_inc(xst, 1)

            copy_agg(0)
            act.wait_ge(bias, NCH)
            relu(0)
            with act.Fori(0, NW - 1) as w:
                act.wait_ge(hid_ps, w + 1)
                copy_agg(w + 1)
                norm(w)
                relu(w + 1)
            norm(NW - 1)

        @block.vector
        def _(dve):
            dve.wait_ge(loaded, 16 * 8)
            with dve.Fori(0, NW) as w:
                chain = Chain(dve, steps, PER, w)
                xw = x1[:, bass.ds(w, 1), :].rearrange("p a f -> p (a f)")
                dve.wait_ge(y_ps, w + 1)
                chain(dve.tensor_tensor(res[:, :], bank[3][:, 0:FEAT], b2b[:, :], ALU.add), wait=True)
                chain(dve.tensor_tensor(res[:, :], res[:, :], xw, ALU.add), wait=True)
                chain(dve.bn_stats(stats[:, :], res[:, :]), wait=True)
                dve.sem_inc(stats_done, 1)
                chain(dve.bn_aggr(mv[:, :], stats[:, :]), wait=True)
                dve.wait_ge(stdev, w + 1)
                chain(dve.reciprocal(std[:, :], std[:, :]), wait=True)
                chain(dve.tensor_scalar(xs[:, :], res[:, :], mv[:, 0:1], std[:, 0:1], ALU.subtract, ALU.mult))
                dve.wait_ge(proj_ps, w + 1)
                dve.wait_ge(stored, 16 * w)
                store_projections(dve, chain, m, 0, w, bank[5], kv_out, prod[:, :])


def attend_stage(nc, m, layer):
    (q_all, acc_all, ring, bank, ident, identb, sel, ew_sb, src_sb) = (m[k] for k in (
        "q_all", "acc_all", "ring", "bank", "ident", "identb", "sel", "ew_sb", "src_sb"))
    kv_rows = m["kv"][layer]
    LAG = 1
    CREDIT = 2 * SLOTS - 2
    with ExitStack() as c:
        def sb(name, shape, dt=F32):
            return c.enter_context(nc.sbuf_tensor(f"a{layer}_{name}", shape, dt))

        idx = sb("idx", [P, SLOTS, BODY], I32)
        hotb = [sb(f"hotb{s}", [P, HALF, P], BF16) for s in (0, 1)]
        hotf = [sb(f"hotf{s}", [P, HALF, P]) for s in (0, 1)]
        hot_t = [sb(f"hot_t{s}", [P, HALF, P]) for s in (0, 1)]
        hot_tb = [sb(f"hot_tb{s}", [P, HALF, P], BF16) for s in (0, 1)]
        mask = [sb(f"mask{s}", [P, HALF, P], BF16) for s in (0, 1)]
        prod = sb("prod", [P, HALF, FEAT])
        dots = sb("dots", [P, HALF, HEADS])
        ewq = sb("ewq", [P, HALF, HEADS])
        score = [sb(f"score{s}", [P, P]) for s in (0, 1)]
        score_t = [sb(f"score_t{s}", [P, P], BF16) for s in (0, 1)]
        maxes = [sb(f"maxes{s}", [P, 1 + HALF, HEADS], BF16) for s in (0, 1)]
        fall = sb("fall", [P, HEADS])
        decay = sb("decay", [P, HEADS])
        shifted = sb("shifted", [P, HALF, HEADS])
        pay = [sb(f"pay{s}", [P, HALF, HEADS, HP]) for s in (0, 1)]
        acc = sb("acc", [P, HEADS, HP])
        zero = sb("zero", [P, 1])
        landed = [c.enter_context(nc.semaphore(f"a{layer}_landed{k}")) for k in range(SLOTS)]
        (rows_ready, idx_there, begun, filled, hot, hotted, turned_ps, turned, masked, narrowed, q_ps, prodded, dotted,
         ewq_there, scored, score_ps, score_tr, spread, maxed, new_max, falls, decayed, max_ps, shifts, weighed,
         valued, edged, summed, shrunk, added, flushed, reset) = (
            c.enter_context(nc.semaphore(f"a{layer}_{n}")) for n in (
                "rows_ready", "idx_there", "begun", "filled", "hot", "hotted", "turned_ps", "turned", "masked", "narrowed", "q_ps",
                "prodded", "dotted", "ewq_there", "scored", "score_ps", "score_tr", "spread", "maxed", "new_max",
                "falls", "decayed", "max_ps", "shifts", "weighed", "valued", "edged", "summed", "shrunk", "added",
                "flushed", "reset"))
        block = c.enter_context(nc.Block())

        def q_bank(s):
            return bank[2 + s][:, 0:HALF * QW].rearrange("p (t q) -> p t q", t=HALF)

        def max_bank(s):
            return bank[4][:, 2 * P + s * HALF * HEADS:2 * P + (s + 1) * HALF * HEADS]

        @block.gpsimd
        def _(pool):
            def gather(k, i, t):
                pool.wait_ge(valued, 2 * i)
                pool.tensor_copy(idx[:, k, :], src_sb[:, bass.ds(t, BODY)]).then_inc(idx_there, 1)
                pool.wait_ge(idx_there, i + 1)
                pool.sem_inc(begun, 1)
                for n in range(BODY):
                    pool.indirect_dma_start(
                        out=ring[:, k, n, :], out_offset=None, in_=kv_rows[:, :],
                        in_offset=bass.IndirectOffsetOnAxis(ap=idx[:, k, n:n + 1], axis=0)).then_inc(landed[k], 16)

            total, first_tile, one, tell = fill_ring(pool, m, NW, LAG, gather, landed, 16 * BODY, rows_ready)
            one(total, (total, first_tile))
            tell(total + SLOTS)

        @block.vector
        def _(dve):
            def products(s, near):
                i = near[0]
                nth = 2 * i + s + 1
                dve.wait_ge(q_ps, nth)
                if s == 0:
                    dve.wait_ge(rows_ready, i + 1 + LAG)
                dve.tensor_tensor(prod[:, :, :], q_bank(s)[:, :, 0:FEAT],
                                  ring[:, bass.ds(i % SLOTS, 1), HALF * s:HALF * (s + 1), 0:FEAT]
                                  .rearrange("p a t f -> p (a t) f"), ALU.mult).then_inc(prodded, 1)
                dve.wait_ge(prodded, nth)
                dve.tensor_reduce(dots[:, :, :].rearrange("p t h -> p (t h)"),
                                  prod[:, :, :].rearrange("p t (h c) -> p (t h) c", h=HEADS), AX.X,
                                  ALU.add).then_inc(dotted, 1)

                t = m["tile_of"](i, near[2], dve)
                dve.tensor_tensor(ewq[:, :, :], q_bank(s)[:, :, FEAT:QW],
                                  repeat(ew_sb[:, bass.ds(t + HALF * s, HALF)].unsqueeze(2), 2, HEADS),
                                  ALU.mult).then_inc(ewq_there, 1)

            def scores(s, near):
                nth = 2 * near[0] + s + 1
                dve.wait_ge(ewq_there, nth)
                dve.wait_ge(dotted, nth)
                dve.tensor_tensor(score[s][:, 0:HALF * HEADS], dots[:, :, :].rearrange("p t h -> p (t h)"),
                                  ewq[:, :, :].rearrange("p t h -> p (t h)"), ALU.add).then_inc(scored, 1)

            def first(now):
                for buf, value in ((score[0][:, :], 0.0), (score[1][:, :], 0.0), (acc[:, :, :], 0.0),
                                   (bank[7][:, 0:PW], 0.0)):
                    dve.memset(buf, value).then_inc(filled, 1)
                dve.wait_ge(filled, 4)
                dve.sem_inc(valued, CREDIT)
                for s in (0, 1):
                    make_onehot(dve, m, hotb[s], s, now).then_inc(hot, 1)
                products(0, now)
                scores(0, now)

            def step(s, now, near, far):
                i, w, row = now
                g = 2 * i + s
                products(1 - s, near)
                dve.wait_ge(hotted, g + 1)
                make_onehot(dve, m, hotb[s], s, far).then_inc(hot, 1)
                scores(1 - s, near)
                for k in range(HALF):
                    dve.wait_ge(spread, HALF * g + k + 1)
                    dve.tensor_reduce(maxes[s][:, 1 + k, :],
                                      bank[5 + k][:, :].rearrange("p (h e) -> p h e", h=HEADS), AX.X,
                                      ALU.max).then_inc(maxed, 1)
                dve.wait_ge(maxed, HALF * g + HALF)
                dve.wait_ge(reset, w + 1)
                dve.tensor_reduce(maxes[1 - s][:, 0, :], maxes[s][:, :, :].rearrange("p k h -> p h k"), AX.X,
                                  ALU.max).then_inc(new_max, 1)
                dve.wait_ge(new_max, g + 1)
                dve.tensor_tensor(fall[:, :], maxes[s][:, 0, :], maxes[1 - s][:, 0, :],
                                  ALU.subtract).then_inc(falls, 1)
                dve.wait_ge(summed, g)
                dve.wait_ge(shrunk, g)
                dve.tensor_tensor(acc[:, :, :].rearrange("p h c -> p (h c)"),
                                  acc[:, :, :].rearrange("p h c -> p (h c)"), bank[7][:, 0:PW],
                                  ALU.add).then_inc(added, 1)
                dve.wait_ge(max_ps, g + 1)
                dve.tensor_tensor(shifted[:, :, :].rearrange("p t h -> p (t h)"), score[s][:, 0:HALF * HEADS],
                                  max_bank(s), ALU.subtract).then_inc(shifts, 1)
                dve.wait_ge(decayed, g + 1)
                dve.wait_ge(added, g + 1)
                dve.tensor_tensor(acc[:, :, :], acc[:, :, :], repeat(decay[:, :].unsqueeze(2), 2, HP),
                                  ALU.mult).then_inc(shrunk, 1)
                dve.wait_ge(weighed, g + 1)
                weight = pay[s][:, :, :, HC:HC + 1]
                t = m["tile_of"](i, row, dve)
                dve.tensor_tensor(pay[s][:, :, :, HC + 1:HP].rearrange("p t h a -> p t (h a)"),
                                  weight.rearrange("p t h a -> p t (h a)"),
                                  repeat(ew_sb[:, bass.ds(t + HALF * s, HALF)].unsqueeze(2), 2, HEADS),
                                  ALU.mult).then_inc(edged, 1)
                v = ring[:, bass.ds(i % SLOTS, 1), HALF * s:HALF * (s + 1), FEAT:2 * FEAT]
                dve.tensor_tensor(pay[s][:, :, :, 0:HC], v.rearrange("p a t (h c) -> p (a t) h c", h=HEADS),
                                  repeat(weight, 3, HC), ALU.mult).then_inc(valued, 1)

            def end(w, halves):
                dve.wait_ge(filled, 4)
                dve.memset(maxes[0][:, 0, :], -2 * BIG).then_inc(reset, 1)
                dve.wait_ge(summed, halves)
                dve.wait_ge(shrunk, halves)
                dve.tensor_tensor(acc_all[:, bass.ds(w, 1), :].rearrange("p a c -> p (a c)"),
                                  acc[:, :, :].rearrange("p h c -> p (h c)"), bank[7][:, 0:PW],
                                  ALU.add).then_inc(flushed, 1)

            in_halves(dve, m, first, step, end)

        @block.tensor
        def _(pe):
            def turn(s, nth):
                pe.wait_ge(hot, nth)
                for k in range(HALF):
                    last = pe.matmul(bank[s][:, k * P:(k + 1) * P], hotb[s][:, k, :], identb[:, :], start=True, stop=True)
                last.then_inc(turned_ps, 1)

            def fetch_q(s, nth, w):
                pe.wait_ge(turned, nth)
                q = q_all[:, bass.ds(w, 1), :].rearrange("p a q -> p (a q)")
                for k in range(HALF):
                    last = pe.matmul(q_bank(s)[:, k, :], hot_t[s][:, k, :], q, start=True, stop=True)
                last.then_inc(q_ps, 1)

            def turn_scores(s, nth):
                pe.wait_ge(scored, nth)
                pe.transpose(bank[4][:, s * P:(s + 1) * P], score[s][:, :], ident[:, :]).then_inc(score_ps, 1)

            def spread_scores(s, nth):
                pe.wait_ge(masked, nth)
                pe.wait_ge(score_tr, nth)
                for k in range(HALF):
                    pe.matmul(bank[5 + k][:, :], identb[:, :], repeat(mask[s][:, k, :].unsqueeze(1), 1, HEADS),
                              start=True, stop=False)
                    for h in range(HEADS):
                        last = pe.matmul(bank[5 + k][:, h * P:(h + 1) * P], sel[:, k * HEADS + h, :],
                                         score_t[s][:, :], start=False, stop=(h == HEADS - 1))
                    last.then_inc(spread, 1)

            def first(now):
                for s in (0, 1):
                    turn(s, s + 1)
                    fetch_q(s, s + 1, 0)
                turn_scores(0, 1)
                spread_scores(0, 1)

            def step(s, now, near, far):
                g = 2 * now[0] + s
                pe.wait_ge(narrowed, g + 1)
                turn(s, g + 3)
                turn_scores(1 - s, g + 2)
                fetch_q(s, g + 3, far[1])
                pe.wait_ge(score_tr, g + 2)
                pe.wait_ge(new_max, g + 1)
                for k in range(HALF):
                    last = pe.matmul(max_bank(s)[:, k * HEADS:(k + 1) * HEADS], hot_tb[s][:, k, :],
                                     maxes[1 - s][:, 0, :], start=True, stop=True)
                last.then_inc(max_ps, 1)
                spread_scores(1 - s, g + 2)
                pe.wait_ge(valued, CREDIT + g + 1)
                pe.wait_ge(edged, g + 1)
                pe.wait_ge(hotted, g + 1)
                pe.wait_ge(added, g + 1)
                for k in range(HALF):
                    last = pe.matmul(bank[7][:, 0:PW], hotf[s][:, k, :],
                                     pay[s][:, k, :, :].rearrange("p h c -> p (h c)"),
                                     start=(k == 0), stop=(k == HALF - 1))
                last.then_inc(summed, 1)

            in_halves(pe, m, first, step, lambda w, halves: None)

        @block.scalar
        def _(act):
            def widen(s, nth):
                act.wait_ge(hot, nth)
                act.activation(hotf[s][:, :, :], hotb[s][:, :, :], ACT.Copy).then_inc(hotted, 1)

            def copy_turned(s, nth):
                act.wait_ge(turned_ps, nth)
                here = bank[s][:, 0:HALF * P]
                act.activation(hot_t[s][:, :, :].rearrange("p t e -> p (t e)"), here, ACT.Copy).then_inc(turned, 1)
                act.activation(mask[s][:, :, :].rearrange("p t e -> p (t e)"), here, ACT.Copy, scale=BIG,
                               bias=-BIG).then_inc(masked, 1)

            def narrow(s):
                act.activation(hot_tb[s][:, :, :].rearrange("p t e -> p (t e)"), bank[s][:, 0:HALF * P],
                               ACT.Copy).then_inc(narrowed, 1)

            def copy_scores(s, nth):
                act.wait_ge(score_ps, nth)
                act.activation(score_t[s][:, :], bank[4][:, s * P:(s + 1) * P], ACT.Copy).then_inc(score_tr, 1)

            def first(now):
                act.activation(zero[:, :], m["epst"][:, :], ACT.Exp)
                for s in (0, 1):
                    copy_turned(s, s + 1)
                    narrow(s)
                widen(0, 1)
                copy_scores(0, 1)

            def step(s, now, near, far):
                g = 2 * now[0] + s
                act.wait_ge(summed, g)
                widen(1 - s, g + 2)
                act.wait_ge(spread, HALF * g + HALF)
                copy_turned(s, g + 3)
                copy_scores(1 - s, g + 2)
                act.wait_ge(falls, g + 1)
                act.wait_ge(shrunk, g)
                act.activation(decay[:, :], fall[:, :], ACT.Exp).then_inc(decayed, 1)
                act.wait_ge(shifts, g + 1)
                act.activation(pay[s][:, :, :, HC:HC + 1].rearrange("p t h a -> p t (h a)"), shifted[:, :, :],
                               ACT.Exp).then_inc(weighed, 1)
                narrow(s)

            in_halves(act, m, first, step, lambda w, halves: None)


def project_stage(nc, m):
    bank, ident, s_all, acc_all = (m[k] for k in ("bank", "ident", "s_all", "acc_all"))
    PER_WINDOW = 5
    PER_GROUP = 6 + OUTW * PER_WINDOW
    with ExitStack() as c:
        def sb(name, shape, dt=F32):
            return c.enter_context(nc.sbuf_tensor(f"p_{name}", shape, dt))

        rden = sb("rden", [P, OUTW * HEADS])
        msg = sb("msg", [P, OUTW, FEAT])
        h_t = [sb(f"h_t{k}", [FEAT, P]) for k in (0, 1)]
        kv_out = [sb(f"kv_out{k}", [P, 2 * FEAT]) for k in (0, 1)]
        prod = sb("prod", [P, FEAT])
        steps, ht_ps, ht, proj_ps, stored0, stored1 = (
            c.enter_context(nc.semaphore(f"p_{n}")) for n in
            ("steps", "ht_ps", "ht", "proj_ps", "stored0", "stored1"))
        stored = (stored0, stored1)
        block = c.enter_context(nc.Block())

        @block.vector
        def _(dve):
            with dve.Fori(0, NW // OUTW) as group:
                chain = Chain(dve, steps, PER_GROUP, group)
                weigh_messages(dve, chain, m, 0, group * OUTW, rden, msg)
                for n in range(OUTW):
                    dve.wait_ge(proj_ps, group * OUTW + n + 1)
                    dve.wait_ge(stored[n % 2], group * (16 * OUT_OF[n % 2]) + 16 * (n // 2))
                    store_projections(dve, chain, m, 1, group * OUTW + n, bank[2 + n % 2], kv_out[n % 2], prod[:, :])

        @block.tensor
        def _(pe):
            with pe.Fori(0, NW // OUTW) as group:
                for n in range(OUTW):
                    nth = group * OUTW + n
                    if n == 0:
                        pe.wait_ge(steps, group * PER_GROUP + 6)
                    else:
                        pe.wait_ge(steps, group * PER_GROUP + 6 + max(n - 1, 0) * PER_WINDOW)
                    pe.transpose(bank[n % 2][:, 0:P], msg[:, n, :], ident[:, :]).then_inc(ht_ps, 1)
                    pe.wait_ge(ht, nth + 1)
                    pe.matmul(bank[2 + n % 2][:, :], h_t[n % 2][:, :], m["wcat"][1][:, :], start=True,
                              stop=True).then_inc(proj_ps, 1)

        @block.scalar
        def _(act):
            with act.Fori(0, NW // OUTW) as group:
                for n in range(OUTW):
                    act.wait_ge(ht_ps, group * OUTW + n + 1)
                    act.activation(h_t[n % 2][:, :], bank[n % 2][:, 0:P], ACT.Relu).then_inc(ht, 1)

        @block.sync
        def _(sp):
            with sp.Fori(0, NW // OUTW) as group:
                for n in range(OUTW):
                    sp.wait_ge(steps, group * PER_GROUP + 6 + n * PER_WINDOW + 1)
                    sp.dma_start(m["kv"][1][bass.ds((group * OUTW + n) * P, P), :],
                                 kv_out[n % 2][:, :]).then_inc(stored[n % 2], 16)
            for k in (0, 1):
                sp.wait_ge(stored[k], 16 * OUT_OF[k] * (NW // OUTW))


def weigh_messages(dve, chain, m, layer, first, rden, msg):
    slots = bass.ds(first + 1, OUTW)
    acc = m["acc_all"][:, slots, :].rearrange("p w (h c) -> p (w h) c", h=HEADS)
    msg_h = msg[:, :, :].rearrange("p w (h c) -> p (w h) c", h=HEADS)
    chain(dve.tensor_scalar(rden[:, :].unsqueeze(2), acc[:, :, HC:HC + 1], 1e-16, None, ALU.add))
    chain(dve.tensor_tensor(msg[:, :, :].rearrange("p w (h c) -> p w h c", h=HEADS),
                            repeat(m["web"][layer][:, :].rearrange("p (h c) -> p h c", h=HEADS).unsqueeze(1), 1, OUTW),
                            repeat(m["acc_all"][:, slots, :].rearrange("p w (h c) -> p w h c", h=HEADS)
                                   [:, :, :, HC + 1:HP], 3, HC), ALU.mult), wait=True)
    chain(dve.reciprocal(rden[:, :], rden[:, :]))
    chain(dve.tensor_tensor(msg_h, msg_h, acc[:, :, 0:HC], ALU.add), wait=True)
    chain(dve.tensor_tensor(msg_h, msg_h, repeat(rden[:, :].unsqueeze(2), 2, HC), ALU.mult), wait=True)
    chain(dve.tensor_tensor(msg[:, :, :], msg[:, :, :], m["s_all"][:, bass.ds(first, OUTW), :], ALU.add), wait=True)


def output_stage(nc, m):
    x1 = m["x1"]
    PER_GROUP = 6 + 1 + 2 * OUTW + 1 + OUTW
    with ExitStack() as c:
        def sb(name, shape, dt=F32):
            return c.enter_context(nc.sbuf_tensor(f"o_{name}", shape, dt))

        rden = sb("rden", [P, OUTW * HEADS])
        msg = sb("msg", [P, OUTW, FEAT])
        stats = sb("stats", [P, OUTW, 6])
        mv = sb("mv", [P, OUTW, 2])
        std = sb("std", [P, OUTW])
        rows = sb("rows", [P, OUTW, FEAT])
        steps, stdev, stored, seen = (c.enter_context(nc.semaphore(f"o_{n}")) for n in
                                      ("steps", "stdev", "stored", "seen"))
        block = c.enter_context(nc.Block())

        @block.vector
        def _(dve):
            with dve.Fori(0, NW // OUTW) as group:
                chain = Chain(dve, steps, PER_GROUP, group)
                here = bass.ds(group * OUTW, OUTW)
                weigh_messages(dve, chain, m, 1, group * OUTW, rden, msg)
                flat = "p w f -> p (w f)"
                chain(dve.scalar_tensor_tensor(msg[:, :, :].rearrange(flat), msg[:, :, :].rearrange(flat), 0.0,
                                               x1[:, here, :].rearrange(flat), ALU.max, ALU.add), wait=True)
                for n in range(OUTW):
                    chain(dve.bn_stats(stats[:, n, :], msg[:, n, :]))
                dve.wait_ge(steps, chain.base + chain.n)
                dve.sem_inc(seen, 1)
                for n in range(OUTW):
                    chain(dve.bn_aggr(mv[:, n, :], stats[:, n, :]))
                dve.wait_ge(stdev, group + 1)
                chain(dve.reciprocal(std[:, :], std[:, :]), wait=True)
                dve.wait_ge(stored, 16 * group)
                for n in range(OUTW):
                    chain(dve.tensor_scalar(rows[:, n, :], msg[:, n, :], mv[:, n, 0:1], std[:, n:n + 1],
                                            ALU.subtract, ALU.mult), wait=(n == OUTW - 1))

        @block.scalar
        def _(act):
            with act.Fori(0, NW // OUTW) as group:
                act.wait_ge(steps, group * PER_GROUP + 7 + 2 * OUTW)
                act.activation(std[:, :], mv[:, :, 1:2].rearrange("p w a -> p (w a)"), ACT.Sqrt,
                               bias=m["epst"][:, :]).then_inc(stdev, 1)

        @block.sync
        def _(sp):
            out_rows = m["out"].rearrange("(w p) f -> p w f", p=P)
            with sp.Fori(0, NW // OUTW) as group:
                sp.wait_ge(steps, group * PER_GROUP + PER_GROUP)
                sp.dma_start(out_rows[:, bass.ds(group * OUTW, OUTW), :], rows[:, :, :]).then_inc(stored, 16)
            sp.wait_ge(stored, 16 * (NW // OUTW))


_SHAPES = ("x", "x_t", "src_t", "dst_t", "dst_r", "ew_t", "edge_attr", "u_t", "w1", "b1_t", "w2", "b2",
           "wcat1", "bcat1", "we1", "wcat2", "bcat2", "we2")


def kernel(**inp):
    import concourse.bacc as bacc
    from concourse.bass_utils import run_bass_kernel_spmd

    a = {k: np.asarray(v) for k, v in inp.items()}

    def rows(v, n):
        return np.concatenate([v, np.zeros((n - v.shape[0],) + v.shape[1:], v.dtype)])

    def by_tile(v, fill):
        v = np.concatenate([v, np.full(TABLE * P - v.shape[0], fill, v.dtype)])
        return np.ascontiguousarray(v.reshape(TABLE, P).T)

    arrays = {
        "x": rows(a["x"], ROWS),
        "x_t": np.ascontiguousarray(rows(a["x"], ROWS).T),
        "src_t": by_tile(a["src"], 0),
        "dst_t": by_tile(a["dst"], -1),
        "dst_r": np.pad(a["dst"], (0, NT * P - EDGES), mode="edge").reshape(NT, P),
        "ew_t": by_tile(a["edge_weight"], 0),
        "edge_attr": rows(a["edge_attr_128"], TABLE * P),
        "u_t": a["L0_gnn_u"].reshape(GLOB, 1),
        "w1": a["L0_gnn_W1"],
        "b1_t": np.ascontiguousarray(a["L0_gnn_b1"].reshape(NCH, P).T),
        "w2": a["L0_gnn_W2"],
        "b2": a["L0_gnn_b2"].reshape(1, FEAT),
    }
    for n in ("1", "2"):
        w = [a[f"L1_gnn_W{k}{n}"] for k in "qkvs"]
        b = [a[f"L1_gnn_b{k}{n}"] for k in "qkvs"]
        arrays["wcat" + n] = np.concatenate(w, axis=1)
        arrays["bcat" + n] = np.concatenate(b).reshape(1, 4 * FEAT)
        arrays["we" + n] = a["L1_gnn_We" + n].reshape(1, FEAT)

    nc = bacc.Bacc("TRN2", target_bir_lowering=False, num_devices=1)
    args = [nc.dram_tensor(f"in_{k}", arrays[k].shape, mybir.dt.from_np(arrays[k].dtype), kind="ExternalInput").ap()
            for k in _SHAPES]
    out = nc.dram_tensor("out_0", (ROWS, FEAT), F32, kind="ExternalOutput").ap()
    build(nc, *args, out)
    r = run_bass_kernel_spmd(nc, [{f"in_{k}": arrays[k] for k in _SHAPES}], core_ids=[0])
    return r.results[0]["out_0"][:NODES]
```
